# Optimizing a Trainium2 kernel written in Bass

```python
import numpy as np
import jax
import jax.numpy as jnp

def _softmax(x, axis=-1):
    return jax.nn.softmax(x, axis=axis)

def _gelu(x):
    return jax.nn.gelu(x, approximate=True)

def _silu(x):
    return jax.nn.silu(x)

def _sigmoid(x):
    return jax.nn.sigmoid(x)

def _layernorm(x, axis=-1, eps=1e-05):
    m = jnp.mean(x, axis=axis, keepdims=True)
    v = jnp.var(x, axis=axis, keepdims=True)
    return (x - m) / jnp.sqrt(v + eps)

def _scatter_add(tgt, idx, src, axis=0):
    return tgt.at[idx].add(src)

def _segment_sum(src, seg, n):
    return jax.ops.segment_sum(src, seg, n)
kernel_name = 'mk_xattn_ffn_d1_seqx_r4_1bffce'

def setup_inputs(seed: int=0):
    np.random.seed(seed)
    _w = jnp.asarray

    def _rec_inputs():
        import jax
        import jax.numpy as jnp
        _rk = jax.random.key(seed)
        x = -0.0002928 + 1 * jax.random.normal(jax.random.fold_in(_rk, 1), (16, 128, 256), jnp.float32)
        _lenS = 128 - jax.random.randint(jax.random.fold_in(_rk, 7), (16,), 0, max(1, 128 // 4) + 1, jnp.int32)
        _lenS2 = 128 - jax.random.randint(jax.random.fold_in(_rk, 8), (16,), 0, max(1, 128 // 4) + 1, jnp.int32)
        _ctx_1024P = jax.random.normal(jax.random.fold_in(_rk, 11), (16, 16, 256), jnp.float32)
        _ctx_1024c = jax.random.dirichlet(jax.random.fold_in(_rk, 511), 0.3 * jnp.ones((16,), jnp.float32), (16, 128))
        _ctx_1024t = jnp.einsum('bsk,bkd->bsd', _ctx_1024c, _ctx_1024P)
        _ctx_1024t = _ctx_1024t * jax.lax.rsqrt(jnp.mean(jnp.square(_ctx_1024t)) + 1e-12) * 0.953939
        ctx_1024 = -1.39393e-06 + 0.999914 * (_ctx_1024t + 0.3 * jax.random.normal(jax.random.fold_in(_rk, 611), (16, 128, 256), jnp.float32))
        return (x, ctx_1024)
    x, ctx_1024 = _rec_inputs()

    def _L0_xattn_setup():
        import jax, jax.numpy as jnp
        import numpy as np
        HIDDEN = 256
        HEADS = 16
        HEAD_DIM = HIDDEN // HEADS
        key = jax.random.key(seed)
        ks = jax.random.split(key, 11)
        B, S = (2, 512)
        s = 1.0 / np.sqrt(HIDDEN)
        return {'query': jax.random.normal(ks[0], (B, S, HIDDEN), jnp.float32), 'key': jax.random.normal(ks[1], (B, S, HIDDEN), jnp.float32), 'value': jax.random.normal(ks[2], (B, S, HIDDEN), jnp.float32), 'Wq': jax.random.normal(ks[3], (HIDDEN, HIDDEN), jnp.float32) * s, 'bq': jnp.zeros((HIDDEN,), jnp.float32), 'Wk': jax.random.normal(ks[4], (HIDDEN, HIDDEN), jnp.float32) * s, 'bk': jnp.zeros((HIDDEN,), jnp.float32), 'Wv': jax.random.normal(ks[5], (HIDDEN, HIDDEN), jnp.float32) * s, 'bv': jnp.zeros((HIDDEN,), jnp.float32), 'Wo': jax.random.normal(ks[6], (HIDDEN, HIDDEN), jnp.float32) * s, 'bo': jnp.zeros((HIDDEN,), jnp.float32)}
    _L0_xattn_all = _L0_xattn_setup()
    _L0_xattn_in = {k: v for k, v in _L0_xattn_all.items() if k in ('Wq', 'bq', 'Wk', 'bk', 'Wv', 'bv', 'Wo', 'bo')}
    del _L0_xattn_all

    def _L0_ffn_setup():
        import jax, jax.numpy as jnp
        import numpy as np
        B, S, H, F, E = (4, 512, 256, 1024, 8)
        key = jax.random.key(seed)
        ks = jax.random.split(key, 8)
        s = 1.0 / np.sqrt(H)
        sf = 1.0 / np.sqrt(F)
        return {'x': jax.random.normal(ks[0], (B, S, H), jnp.float32), 'wr': jax.random.uniform(ks[1], (H, E), jnp.float32, -s, s), 'br': jax.random.uniform(ks[2], (E,), jnp.float32, -s, s), 'w1': jax.random.uniform(ks[3], (E, H, F), jnp.float32, -s, s), 'b1': jax.random.uniform(ks[4], (E, F), jnp.float32, -s, s), 'w2': jax.random.uniform(ks[5], (E, F, H), jnp.float32, -sf, sf), 'b2': jax.random.uniform(ks[6], (E, H), jnp.float32, -sf, sf)}
    _L0_ffn_all = _L0_ffn_setup()
    _L0_ffn_in = {k: v for k, v in _L0_ffn_all.items() if k in ('wr', 'br', 'w1', 'b1', 'w2', 'b2')}
    del _L0_ffn_all
    return {'x': x, 'ctx_1024': ctx_1024, 'L0_xattn_Wq': _L0_xattn_in['Wq'], 'L0_xattn_bq': _L0_xattn_in['bq'], 'L0_xattn_Wk': _L0_xattn_in['Wk'], 'L0_xattn_bk': _L0_xattn_in['bk'], 'L0_xattn_Wv': _L0_xattn_in['Wv'], 'L0_xattn_bv': _L0_xattn_in['bv'], 'L0_xattn_Wo': _L0_xattn_in['Wo'], 'L0_xattn_bo': _L0_xattn_in['bo'], 'L0_ffn_wr': _L0_ffn_in['wr'], 'L0_ffn_br': _L0_ffn_in['br'], 'L0_ffn_w1': _L0_ffn_in['w1'], 'L0_ffn_b1': _L0_ffn_in['b1'], 'L0_ffn_w2': _L0_ffn_in['w2'], 'L0_ffn_b2': _L0_ffn_in['b2']}

def reference(x, ctx_1024, L0_xattn_Wq, L0_xattn_bq, L0_xattn_Wk, L0_xattn_bk, L0_xattn_Wv, L0_xattn_bv, L0_xattn_Wo, L0_xattn_bo, L0_ffn_wr, L0_ffn_br, L0_ffn_w1, L0_ffn_b1, L0_ffn_w2, L0_ffn_b2):
    import jax
    import jax.numpy as jnp

    def _L0_xattn_ref(query, key, value, Wq, bq, Wk, bk, Wv, bv, Wo, bo):
        import jax, jax.numpy as jnp
        import numpy as np
        HIDDEN = 256
        HEADS = 16
        HEAD_DIM = HIDDEN // HEADS
        B, S, _ = query.shape
        Q = query @ Wq.T + bq
        K = key @ Wk.T + bk
        V = value @ Wv.T + bv
        Q = Q.reshape(B, S, HEADS, HEAD_DIM).transpose(0, 2, 1, 3)
        K = K.reshape(B, S, HEADS, HEAD_DIM).transpose(0, 2, 1, 3)
        V = V.reshape(B, S, HEADS, HEAD_DIM).transpose(0, 2, 1, 3)
        scale = jnp.sqrt(jnp.float32(HEAD_DIM))
        energy = jnp.einsum('bhqd,bhkd->bhqk', Q, K) / scale
        attn = jax.nn.softmax(energy, axis=-1)
        x = jnp.einsum('bhqk,bhkd->bhqd', attn, V)
        x = x.transpose(0, 2, 1, 3).reshape(B, S, HIDDEN)
        return x @ Wo.T + bo

    def _L0_ffn_ref(x, wr, br, w1, b1, w2, b2):
        import jax, jax.numpy as jnp
        import numpy as np
        B, S, H, F, E = (4, 512, 256, 1024, 8)
        scores = jnp.einsum('bsh,he->bse', x, wr) + br
        expert_id = jnp.argmax(scores, axis=-1)
        h = jnp.einsum('bsh,ehf->ebsf', x, w1) + b1[:, None, None, :]
        h = jax.nn.gelu(h, approximate=False)
        y = jnp.einsum('ebsf,efh->ebsh', h, w2) + b2[:, None, None, :]
        one_hot = jax.nn.one_hot(expert_id, E, dtype=x.dtype)
        out = jnp.einsum('ebsh,bse->bsh', y, one_hot)
        return out
    x = x + _L0_xattn_ref(_layernorm(x, axis=-1), ctx_1024, ctx_1024, L0_xattn_Wq, L0_xattn_bq, L0_xattn_Wk, L0_xattn_bk, L0_xattn_Wv, L0_xattn_bv, L0_xattn_Wo, L0_xattn_bo)
    x = x + _L0_ffn_ref(_layernorm(x, axis=-1), L0_ffn_wr, L0_ffn_br, L0_ffn_w1, L0_ffn_b1, L0_ffn_w2, L0_ffn_b2)
    return x

_drawn_inputs = setup_inputs


def setup_inputs(seed=0):
    import zlib

    import numpy as np

    out = dict(_drawn_inputs(seed))
    spreads = {'L0_xattn_bq': (0.0, 0.1),
     'L0_xattn_bk': (0.0, 0.8),
     'L0_xattn_bv': (0.0, 0.1),
     'L0_xattn_bo': (0.0, 0.1)}
    factors = {'L0_ffn_b1': 5.143, 'L0_ffn_b2': 3.612}
    for name, (base, spread) in spreads.items():
        noise = np.random.default_rng([zlib.crc32(name.encode()), seed]).standard_normal(out[name].shape)
        drawn = base * np.exp(spread * noise) if base else spread * noise
        out[name] = jnp.asarray(drawn.astype(out[name].dtype))
    for name, factor in factors.items():
        out[name] = (out[name] * factor).astype(out[name].dtype)
    return out
```

```python
from contextlib import ExitStack

import concourse.bass as bass
from concourse import mybir

ALU = mybir.AluOpType
ACT = mybir.ActivationFunctionType
AX_X = mybir.AxisListType.X
F32 = mybir.dt.float32
F16 = mybir.dt.float16
I32 = mybir.dt.int32


class Batch:

    def __init__(self, half, parity):
        self.half, self.p, self.n = half, parity, half * 2 + parity


def cross_attention_moe_kernel(nc, x, ctxT, wqT, bqT, wkT, bkT, wvT, bv, woT, bo, wr, br, w1, b1T, w2, b2, out):
    NB, S, D = x.shape
    P = 128
    KC = D // P
    HEADS = 16
    HD = D // HEADS
    HG = P // HD
    QUAD = 4
    NQ = HEADS // QUAD
    E, _, F = w1.shape
    FC = F // P
    NTOK = NB * S
    TILES = NTOK // P
    SLOTS = (NTOK + E * (P - 1)) // P
    SLOTS_W = SLOTS + SLOTS % 2
    EPS = 1e-5
    SCALE = float(HD) ** -0.5
    NEWTON_STEPS = 3
    NEWTON_OPS = 3 + 3 * NEWTON_STEPS
    RSQRT_MAGIC = 0x5F3759DF
    OUT_OF_BOUNDS = 2 * NTOK
    assert S == P and D == KC * P and E * TILES == P

    with ExitStack() as ctx:
        def sb(name, shape, dt=F32):
            return ctx.enter_context(nc.sbuf_tensor(name, shape, dt))

        def psum(name, shape, dt=F32):
            return ctx.enter_context(nc.psum_tensor(name, shape, dt))

        def sem(name):
            return ctx.enter_context(nc.semaphore(name))

        w1_sb = sb("w1_sb", [P, E, KC, F])
        w2_sb = sb("w2_sb", [P, E, FC, D])
        b1_sb = sb("b1_sb", [P, E * FC])
        wq_sb = sb("wq_sb", [P, KC, D])
        wk_sb = sb("wk_sb", [P, KC, D])
        wv_sb = sb("wv_sb", [P, KC, D])
        wo_sb = sb("wo_sb", [P, KC, D])
        wr_sb = sb("wr_sb", [P, KC, E])
        bq_sb = sb("bq_sb", [P, KC])
        bk_sb = sb("bk_sb", [P, KC])
        bv_sb = sb("bv_sb", [P, D])
        bo_sb = sb("bo_sb", [P, D])
        br_sb = sb("br_sb", [P, E])
        ident = sb("ident", [P, P])
        before = sb("before", [P, P], F16)
        ones = sb("ones", [P, P], F16)
        iota_i = sb("iota_i", [P, P], I32)
        iota_row = sb("iota_row", [P, P])
        iota_part_i = sb("iota_part_i", [P, 1], I32)
        iota_part = sb("iota_part", [P, 1])
        rev_i = sb("rev_i", [P, E], I32)
        rev = sb("rev", [P, E])
        tok_i = sb("tok_i", [P, NB], I32)
        tok1 = sb("tok1", [P, NB])

        x_sb = sb("x_sb", [P, 2, D])
        xb_sb = sb("xb_sb", [P, 2, D])
        ctx_sb = sb("ctx_sb", [P, 2, KC, P])
        xn = sb("xn", [P, D])
        xnT = sb("xnT", [P, KC, P])
        qT = sb("qT", [P, KC, P])
        kT = sb("kT", [P, KC, P])
        k_diag = sb("k_diag", [P, KC, HG, P])
        v_diag = sb("v_diag", [P, 2, KC, HG, P])
        probs = sb("probs", [P, HEADS, P])
        probsT = sb("probsT", [P, 2, QUAD * P])
        row_max = sb("row_max", [P, HEADS])
        neg_max = sb("neg_max", [P, HEADS])
        sums = sb("sums", [P, 2, HEADS])
        recips = sb("recips", [P, HEADS])
        recips_d = sb("recips_d", [P, HEADS, HD])
        recipsT = sb("recipsT", [P, KC, P])
        oT = sb("oT", [P, 2, KC, P])
        record = sb("record", [P, 2, 2 * D])
        x2T = sb("x2T", [P, KC, P])
        stats = sb("stats", [P, 2, 6])
        mean_var = sb("mean_var", [P, 2, 2])
        nw_y = sb("nw_y", [P, 2])
        nw_i = sb("nw_i", [P, 2], I32)
        nw_v = sb("nw_v", [P, 2])
        nw_t = sb("nw_t", [P, 2])
        nw_u = sb("nw_u", [P, 2])
        logits = sb("logits", [P, E])
        best = sb("best", [P, 1])
        keyed = sb("keyed", [P, E])
        key = sb("key", [P, 1])
        onehot = sb("onehot", [P, 2, E], F16)
        seen = sb("seen", [P, E], F16)
        ranked = sb("ranked", [P, E])
        rank = sb("rank", [P, 1])
        rank_i = sb("rank_i", [P, 1], I32)
        tile_i = sb("tile_i", [P, 1], I32)
        place_i = sb("place_i", [P, 1], I32)
        place = sb("place", [P, 1])
        e_code = sb("e_code", [P, 1])
        code = sb("code", [P, 1])
        place_hot = sb("place_hot", [P, NB, P], F16)
        code_tok = sb("code_tok", [P, NB, P], F16)

        PAD = E
        n_i = sb("n_i", [P, E], I32)
        n_sh = sb("n_sh", [P, E], I32)
        n_f = sb("n_f", [P, E])
        ends = sb("ends", [P, 4, PAD + E])
        slot_i = sb("slot_i", [P, SLOTS_W], I32)
        slot_f = sb("slot_f", [P, SLOTS_W])
        passed, passed_n = (probs[:, i:i + 2].rearrange("p h k -> p (h k)")[:, 0:SLOTS_W * E].rearrange(
            "p (s e) -> p s e", e=E) for i in (0, 2))
        slot_e = sb("slot_e", [P, SLOTS_W])
        slot_start = sb("slot_start", [P, SLOTS_W])
        slot_e_i = sb("slot_e_i", [P, SLOTS_W], I32)
        slot_c = sb("slot_c", [P, SLOTS_W])
        slot_code = sb("slot_code", [P, SLOTS_W])
        code_hot = sb("code_hot", [P, SLOTS_W], F16)
        ids_T = sb("ids_T", [P, P], F16)
        ids = sb("ids", [P, SLOTS_W])
        ids_pad = sb("ids_pad", [P, SLOTS_W])
        gather_i = sb("gather_i", [P, SLOTS_W], I32)
        scatter_i = sb("scatter_i", [P, SLOTS_W], I32)
        g_idx = sb("g_idx", [P, 2, 1], I32)
        s_idx = sb("s_idx", [P, 2, 1], I32)

        spare = v_diag[:].rearrange("p b c h s -> p (b c h s)")
        b2_sb = k_diag[:].rearrange("p c h s -> p (c h s)")[:, 0:E * D]
        at = [0]

        def reuse(*shape):
            size = 1
            for n in shape:
                size *= n
            at[0] += size
            return spare[:, at[0] - size:at[0]]

        gathered = reuse(2, 2 * D).rearrange("p (b d) -> p b d", b=2)
        xeT = reuse(2, KC, P).rearrange("p (b c s) -> p b c s", b=2, c=KC)
        h_sb = reuse(F)
        hT = reuse(FC, P).rearrange("p (c s) -> p c s", c=FC)
        y_sb = reuse(2, D).rearrange("p (b d) -> p b d", b=2)

        banks = [psum(f"bank{i}", [P, 512]) for i in range(8)]
        S_BANK, T_BANK = banks[0:4], banks[4:6]
        BANK_A, BANK_B = banks[6], banks[7]

        records = nc.dram_tensor("records", [NTOK, 2 * D], F32).ap()

        names = """consts_pool consts_dve wq_in wk_in wv_in wo_in wr_in bias_in w1_in w2_in
            xb_done k_ready k_taken v_ready v_taken xT_ready xT_taken q_ready q_taken
            stats1 aggr1 stats2 aggr2 newton xn_done xn2_done scores_ready max_done neg_done exp_done
            probsT_ready probsT_taken values_weighed recip_done recip_d_done rT_ready rT_taken oT_done
            y_ready x1_done x2T_ready x2T_taken logits_ready logits_taken best_done keyed_done key_done
            onehot_done rank_ready ranked_done rank_done seen_done rank_i_done split_done code_done
            hot_done total_ready table ids_T_ready ids_T_done ids_ready index_done slots_done
            idx_copied scattered xeT_ready xeT_taken h_ready h_taken hT_ready gelu_done ye_ready ye_done
            b2_done b2_in""".split()
        sm = {n: sem(n) for n in names}
        x_in = [sem("x_in0"), sem("x_in1")]
        ctx_in = [sem("ctx_in0"), sem("ctx_in1")]
        kdiag_in = [sem("kdiag_in0"), sem("kdiag_in1")]
        record_out = [sem("record_out0"), sem("record_out1")]
        gathered_in = [sem("gathered_in0"), sem("gathered_in1")]
        y_out = [sem("y_out0"), sem("y_out1")]

        KDIAG_DMAS = HG

        def held(eng, value):
            return value if isinstance(value, int) else eng.to_reg(value)

        def steps(eng, first, step, last):
            first()
            step(Batch(0, 0), Batch(0, 1), None)
            with eng.Fori(0, NB // 2 - 1) as j:
                step(Batch(j, 1), Batch(j + 1, 0), Batch(j, 0))
                step(Batch(j + 1, 0), Batch(j + 1, 1), Batch(j, 1))
            step(Batch(NB // 2 - 1, 1), None, Batch(NB // 2 - 1, 0))
            last(Batch(NB // 2 - 1, 1))

        def slots(eng, body):
            with eng.Fori(0, SLOTS // 2) as j:
                body(j * 2, 0, j)
                body(j * 2 + 1, 1, j)
            if SLOTS % 2:
                body(SLOTS - 1, 0, SLOTS // 2)

        block = ctx.enter_context(nc.Block())

        @block.sync
        def _(sp):
            def load(b):
                sp.dma_start(ctx_sb[:, b.p], ctxT[bass.ds(b.n, 1)].rearrange("o (c p) s -> p (o c) s", p=P)).then_inc(ctx_in[b.p], 16)
                sp.dma_start(x_sb[:, b.p], x[bass.ds(b.n, 1)].rearrange("o p d -> p (o d)")).then_inc(x_in[b.p], 16)

            def k_blocks(b):
                taken, scored = held(sp, b.n + 1), held(sp, b.n * NQ)
                sp.wait_ge(sm["consts_pool"], 3)
                sp.wait_ge(sm["k_taken"], taken)
                if not (isinstance(b.n, int) and b.n == 0):
                    sp.wait_ge(sm["scores_ready"], scored)
                for h in range(HG):
                    rows = slice(HD * h, HD * (h + 1))
                    sp.dma_start(k_diag[rows, :, h, :], kT[rows]).then_inc(kdiag_in[b.p], 16)

            def save_record(b):
                sp.wait_ge(sm["xn2_done"], b.n + 1)
                sp.dma_start(records[bass.ds(b.n * P, P), :], record[:, b.p]).then_inc(record_out[b.p], 16)

            def first():
                load(Batch(0, 0))
                for name, dst, src in (("wk_in", wk_sb, wkT), ("wv_in", wv_sb, wvT), ("wq_in", wq_sb, wqT)):
                    sp.dma_start(dst[:], src.rearrange("(c p) n -> p c n", p=P)).then_inc(sm[name], 16)
                load(Batch(0, 1))
                sp.dma_start(wo_sb[:], woT.rearrange("(c p) n -> p c n", p=P)).then_inc(sm["wo_in"], 16)
                sp.dma_start(wr_sb[:], wr.rearrange("(c p) e -> p c e", p=P)).then_inc(sm["wr_in"], 16)
                k_blocks(Batch(0, 0))

            def step(b, nxt, prev):
                if nxt is not None and not (isinstance(b.n, int) and b.n + 2 >= NB):
                    after = Batch(b.half + 1, b.p)
                    sp.wait_ge(sm["v_ready"], b.n + 1)
                    sp.wait_ge(sm["xn_done"], b.n + 1)
                    sp.wait_ge(sm["xb_done"], b.n + 1)
                    load(after)
                if nxt is not None:
                    k_blocks(nxt)
                if prev is not None:
                    save_record(prev)

            first()
            step(Batch(0, 0), Batch(0, 1), None)
            with sp.Fori(0, NB // 2 - 2) as j:
                step(Batch(j, 1), Batch(j + 1, 0), Batch(j, 0))
                step(Batch(j + 1, 0), Batch(j + 1, 1), Batch(j, 1))
            h = NB // 2 - 2
            step(Batch(h, 1), Batch(h + 1, 0), Batch(h, 0))
            k_blocks(Batch(h + 1, 1))
            save_record(Batch(h, 1))
            save_record(Batch(h + 1, 0))
            save_record(Batch(h + 1, 1))
            sp.dma_start(b2_sb, b2.rearrange("(o n) -> o n", o=1).broadcast_to([P, E * D])).then_inc(sm["b2_in"], 16)

        @block.gpsimd
        def _(pool):
            g = nc.gpsimd
            g.memset(k_diag[:], 0.0)
            g.memset(v_diag[:], 0.0)
            g.memset(ident[:], 0.0)
            g.memset(before[:], 1.0)
            g.memset(seen[:], 0.0).then_inc(sm["consts_pool"], 1)
            pool.wait_ge(sm["consts_pool"], 1)
            g.affine_select(out=ident[:], in_=ident[:], compare_op=ALU.not_equal, fill=1.0, base=0,
                            pattern=[[-1, P]], channel_multiplier=1)
            g.affine_select(out=before[:], in_=before[:], compare_op=ALU.is_ge, fill=0.0, base=-1,
                            pattern=[[1, P]], channel_multiplier=-1)
            g.memset(ones[:], 1.0)
            g.iota(iota_i[:], pattern=[[1, P]], base=0, channel_multiplier=0)
            g.iota(iota_part_i[:], pattern=[[1, 1]], base=0, channel_multiplier=1)
            g.iota(rev_i[:], pattern=[[-1, E]], base=E, channel_multiplier=0)
            g.iota(tok_i[:], pattern=[[P, NB]], base=1, channel_multiplier=1)
            g.iota(slot_i[:], pattern=[[1, SLOTS_W]], base=0, channel_multiplier=0).then_inc(sm["consts_pool"], 1)
            pool.wait_ge(sm["consts_pool"], 2)
            g.tensor_copy(iota_row[:], iota_i[:])
            g.tensor_copy(iota_part[:], iota_part_i[:])
            g.tensor_copy(rev[:], rev_i[:])
            g.tensor_copy(tok1[:], tok_i[:])
            g.tensor_copy(slot_f[:], slot_i[:]).then_inc(sm["consts_pool"], 1)

            def add_bo(b, used):
                pool.wait_ge(x_in[b.p], (b.half + 1) * 16)
                if used is not None:
                    pool.wait_ge(sm["x1_done"], used.n + 1)
                g.tensor_tensor(xb_sb[:, b.p], x_sb[:, b.p], bo_sb[:], ALU.add).then_inc(sm["xb_done"], 1)

            pool.wait_ge(sm["bias_in"], 16 * 6)
            add_bo(Batch(0, 0), None)
            add_bo(Batch(0, 1), None)
            with pool.Fori(0, NB // 2 - 1) as j:
                add_bo(Batch(j + 1, 0), Batch(j, 0))
                add_bo(Batch(j + 1, 1), Batch(j, 1))

            def scatter(s, p, j):
                g.tensor_copy(s_idx[:, p], scatter_i[:, bass.ds(s, 1)]).then_inc(sm["scattered"], 1)
                count = held(pool, s + 1)
                pool.wait_ge(sm["index_done"], 2)
                pool.wait_ge(sm["scattered"], count)
                pool.wait_ge(sm["ye_done"], count)
                g.indirect_dma_start(out=out[:, :], out_offset=bass.IndirectOffsetOnAxis(ap=s_idx[:, p], axis=0),
                                     in_=y_sb[:, p], in_offset=None, bounds_check=NTOK - 1, oob_is_err=False)\
                    .then_inc(y_out[p], 16)

            def gather(s, p, wait_used=True):
                if wait_used:
                    pool.wait_ge(sm["ye_done"], s - 1)
                g.tensor_copy(g_idx[:, p], gather_i[:, bass.ds(s, 1)]).then_inc(sm["idx_copied"], 1)
                copied = held(pool, s + 1)
                pool.wait_ge(sm["index_done"], 2)
                pool.wait_ge(sm["idx_copied"], copied)
                g.indirect_dma_start(out=gathered[:, p], out_offset=None, in_=records[:, :],
                                     in_offset=bass.IndirectOffsetOnAxis(ap=g_idx[:, p], axis=0))\
                    .then_inc(gathered_in[p], 16)

            pool.wait_ge(sm["index_done"], 2)
            for p in range(2):
                pool.wait_ge(record_out[p], 16 * (NB // 2))
            gather(0, 0, False)
            gather(1, 1, False)
            with pool.Fori(0, (SLOTS - 2) // 2) as j:
                scatter(j * 2, 0, j)
                gather(j * 2 + 2, 0)
                scatter(j * 2 + 1, 1, j)
                gather(j * 2 + 3, 1)
            done = (SLOTS - 2) // 2 * 2
            for s in range(done, SLOTS):
                scatter(s, s % 2, s // 2)
                if s + 2 < SLOTS:
                    gather(s + 2, s % 2)
            pool.wait_ge(y_out[0], 16 * ((SLOTS + 1) // 2))
            pool.wait_ge(y_out[1], 16 * (SLOTS // 2))

        @block.scalar
        def _(act):
            a = nc.scalar

            def rep(v, n):
                return v.rearrange("(o n) -> o n", o=1).broadcast_to([P, n])

            act.dma_start(bk_sb[:], bkT).then_inc(sm["bias_in"], 16)
            act.dma_start(bq_sb[:], bqT).then_inc(sm["bias_in"], 16)
            act.dma_start(bv_sb[:], rep(bv, D)).then_inc(sm["bias_in"], 16)
            act.dma_start(bo_sb[:], rep(bo, D)).then_inc(sm["bias_in"], 16)
            act.dma_start(br_sb[:], rep(br, E)).then_inc(sm["bias_in"], 16)
            act.dma_start(b1_sb[:], b1T).then_inc(sm["bias_in"], 16)
            for e in range(E):
                act.dma_start(w1_sb[:, e], w1[e].rearrange("(c p) f -> p c f", p=P)).then_inc(sm["w1_in"], 16)
                act.dma_start(w2_sb[:, e], w2[e].rearrange("(c p) d -> p c d", p=P)).then_inc(sm["w2_in"], 16)

            def exps(b, q):
                act.wait_ge(sm["neg_done"], b.n * NQ + (q + 1))
                for i in range(QUAD):
                    h = QUAD * q + i
                    ins = a.activation(probs[:, h], S_BANK[q][:, P * i:P * (i + 1)], ACT.Exp, scale=SCALE,
                                       bias=neg_max[:, h:h + 1], accum_out=sums[:, b.p, h:h + 1])
                ins.then_inc(sm["exp_done"], 1)

            def take_k(b, prev):
                act.wait_ge(sm["k_ready"], b.n + 1)
                if prev is not None:
                    act.wait_ge(kdiag_in[prev.p], (prev.half + 1) * (16 * KDIAG_DMAS))
                for c in range(KC):
                    ins = a.activation(kT[:, c], BANK_B[:, P * c:P * (c + 1)], ACT.Identity,
                                       bias=bk_sb[:, c:c + 1])
                ins.then_inc(sm["k_taken"], 1)

            def take_xT(b):
                act.wait_ge(sm["xT_ready"], b.n + 1)
                a.copy(xnT[:], BANK_B[:, 0:D].rearrange("p (c s) -> p c s", c=KC)).then_inc(sm["xT_taken"], 1)

            def take_q(b):
                act.wait_ge(sm["q_ready"], b.n + 1)
                for c in range(KC):
                    ins = a.activation(qT[:, c], BANK_B[:, P * c:P * (c + 1)], ACT.Identity,
                                       bias=bq_sb[:, c:c + 1])
                ins.then_inc(sm["q_taken"], 1)

            def take_x2T(b):
                act.wait_ge(sm["x2T_ready"], b.n + 1)
                a.copy(x2T[:], BANK_A[:, 0:D].rearrange("p (c s) -> p c s", c=KC)).then_inc(sm["x2T_taken"], 1)

            def take_probsT(b, q):
                act.wait_ge(sm["probsT_ready"], b.n * NQ + (q + 1))
                if q >= 2:
                    act.wait_ge(sm["values_weighed"], b.n * NQ + (q - 1))
                elif not (isinstance(b.n, int) and b.n == 0):
                    act.wait_ge(sm["values_weighed"], b.n * NQ + (q - 1))
                a.copy(probsT[:, q % 2], T_BANK[q % 2][:]).then_inc(sm["probsT_taken"], 1)

            def take_rT(b):
                act.wait_ge(sm["rT_ready"], b.n + 1)
                a.copy(recipsT[:], BANK_B[:, 0:D].rearrange("p (c s) -> p c s", c=KC)).then_inc(sm["rT_taken"], 1)

            def first():
                act.wait_ge(sm["bias_in"], 16 * 6)
                take_k(Batch(0, 0), None)
                take_xT(Batch(0, 0))
                take_q(Batch(0, 0))

            def step(b, nxt, prev):
                for q in range(NQ - 1):
                    exps(b, q)
                if nxt is not None:
                    take_k(nxt, b)
                exps(b, NQ - 1)
                if nxt is not None:
                    take_xT(nxt)
                if prev is not None:
                    take_x2T(prev)
                take_probsT(b, 0)
                if nxt is not None:
                    take_q(nxt)
                for q in range(1, NQ):
                    take_probsT(b, q)
                take_rT(b)

            def last(b):
                take_x2T(b)

            steps(act, first, step, last)

            with nc.scalar.register("slot_expert_act") as reg:
                def expert_gelu(s, p, j):
                    a.reg_load(reg, slot_e_i[0:1, bass.ds(s, 1)])
                    e = nc.s_assert_within(a.snap(reg), 0, E - 1)
                    act.wait_ge(sm["xeT_ready"], s + 1)
                    a.copy(xeT[:, p], BANK_A[:, 0:D].rearrange("p (c s) -> p c s", c=KC)).then_inc(sm["xeT_taken"], 1)
                    for c in range(FC):
                        if c % 4 == 0:
                            act.wait_ge(sm["hT_ready"], s * 2 + (c // 4 + 1))
                        ins = a.activation(hT[:, c], T_BANK[c // 4][:, P * (c % 4):P * (c % 4 + 1)], ACT.Gelu,
                                           bias=b1_sb[:, bass.ds(e * FC + c, 1)])
                        if c % 4 == 3:
                            ins.then_inc(sm["gelu_done"], 1)
                act.wait_ge(sm["slots_done"], 1)
                slots(act, expert_gelu)

        @block.vector
        def _(dve):
            v = nc.vector
            LN2, LN1 = 0, 1

            def stats_of(src, col, name, count):
                count = held(dve, count)
                v.bn_stats(stats[:, col], src).then_inc(sm["stats" + name], 1)
                dve.wait_ge(sm["consts_dve"], 1)
                dve.wait_ge(sm["stats" + name], count)
                v.bn_aggr(mean_var[:, col], stats[:, col]).then_inc(sm["aggr" + name], 1)

            def stats_x(b):
                dve.wait_ge(x_in[b.p], (b.half + 1) * 16)
                if not isinstance(b.n, int) or b.n > 0:
                    dve.wait_ge(sm["xn_done"], b.n)
                stats_of(x_sb[:, b.p], LN1, "1", b.n + 1)

            def inverse_roots(turn):
                n = [0]

                def link(ins):
                    n[0] += 1
                    ins.then_inc(sm["newton"], 1)
                    dve.wait_ge(sm["newton"], turn * NEWTON_OPS + n[0])

                link(v.tensor_scalar(nw_v[:], mean_var[:, :, 1], EPS, None, ALU.add))
                link(v.tensor_scalar(nw_i[:], nw_v[:].bitcast(I32), 1, None, ALU.logical_shift_right))
                link(v.tensor_scalar(nw_y[:].bitcast(I32), nw_i[:], -1, RSQRT_MAGIC, ALU.mult, ALU.add))
                for _ in range(NEWTON_STEPS):
                    link(v.tensor_tensor(nw_t[:], nw_y[:], nw_y[:], ALU.mult))
                    link(v.scalar_tensor_tensor(out=nw_u[:], in0=nw_t[:], scalar=-0.5, in1=nw_v[:],
                                                op0=ALU.mult, op1=ALU.mult))
                    link(v.scalar_tensor_tensor(out=nw_y[:], in0=nw_u[:], scalar=1.5, in1=nw_y[:],
                                                op0=ALU.add, op1=ALU.mult))

            def normalize(dst, src, col, done):
                v.tensor_scalar(dst, src, mean_var[:, col, 0:1], nw_y[:, col:col + 1],
                                ALU.subtract, ALU.mult).then_inc(done, 1)

            def maxima(b, q):
                dve.wait_ge(sm["scores_ready"], b.n * NQ + (q + 1))
                hs = slice(QUAD * q, QUAD * (q + 1))
                v.tensor_reduce(row_max[:, hs], S_BANK[q][:].rearrange("p (h k) -> p h k", k=P), AX_X,
                                ALU.max).then_inc(sm["max_done"], 1)
                dve.wait_ge(sm["max_done"], b.n * NQ + (q + 1))
                v.tensor_scalar(neg_max[:, hs], row_max[:, hs], -SCALE, None, ALU.mult).then_inc(sm["neg_done"], 1)

            def residual(b):
                dve.wait_ge(sm["y_ready"], b.n + 1)
                dve.wait_ge(sm["xb_done"], b.n + 1)
                if not isinstance(b.n, int) or b.n >= 2:
                    if isinstance(b.n, int):
                        dve.wait_ge(record_out[b.p], b.half * 16)
                    else:
                        dve.wait_ge(record_out[b.p], b.half * 16)
                v.tensor_tensor(record[:, b.p, 0:D], BANK_A[:, 0:D], xb_sb[:, b.p], ALU.add)\
                    .then_inc(sm["x1_done"], 1)
                dve.wait_ge(sm["x1_done"], b.n + 1)
                stats_of(record[:, b.p, 0:D], LN2, "2", b.n + 1)

            def take_v(b):
                dve.wait_ge(sm["v_ready"], b.n + 1)
                for c in range(KC):
                    blocks = v_diag[:, b.p, c].rearrange("p h (i d) -> p (h i) d", d=HD)[:, ::HG + 1, :]
                    ins = v.tensor_tensor(blocks, BANK_A[:, P * c:P * (c + 1)].rearrange("p (h d) -> p h d", d=HD),
                                          bv_sb[:, P * c:P * (c + 1)].rearrange("p (h d) -> p h d", d=HD), ALU.add)
                ins.then_inc(sm["v_taken"], 1)

            def choose(b):
                dve.wait_ge(sm["logits_ready"], b.n + 1)
                v.tensor_tensor(logits[:], BANK_B[:, 0:E], br_sb[:], ALU.add).then_inc(sm["logits_taken"], 1)
                dve.wait_ge(sm["logits_taken"], b.n + 1)
                v.tensor_reduce(best[:], logits[:], AX_X, ALU.max).then_inc(sm["best_done"], 1)
                dve.wait_ge(sm["best_done"], b.n + 1)
                v.scalar_tensor_tensor(out=keyed[:], in0=logits[:], scalar=best[:], in1=rev[:],
                                       op0=ALU.is_equal, op1=ALU.mult).then_inc(sm["keyed_done"], 1)
                dve.wait_ge(sm["keyed_done"], b.n + 1)
                v.tensor_reduce(key[:], keyed[:], AX_X, ALU.max).then_inc(sm["key_done"], 1)
                dve.wait_ge(sm["key_done"], b.n + 1)
                v.tensor_scalar(onehot[:, b.p], rev[:], key[:], None, ALU.is_equal).then_inc(sm["onehot_done"], 1)
                v.tensor_scalar(e_code[:], key[:], -float(TILES), float(E * TILES), ALU.mult, ALU.add)\
                    .then_inc(sm["split_done"], 1)

            def place_tokens(b):
                dve.wait_ge(sm["rank_ready"], b.n + 1)
                v.tensor_tensor(ranked[:], BANK_B[:, 0:E], onehot[:, b.p], ALU.mult).then_inc(sm["ranked_done"], 1)
                v.tensor_tensor(seen[:], seen[:], onehot[:, b.p], ALU.add).then_inc(sm["seen_done"], 1)
                dve.wait_ge(sm["ranked_done"], b.n + 1)
                v.tensor_reduce(rank[:], ranked[:], AX_X, ALU.add).then_inc(sm["rank_done"], 1)
                dve.wait_ge(sm["rank_done"], b.n + 1)
                v.tensor_copy(rank_i[:], rank[:]).then_inc(sm["rank_i_done"], 1)
                dve.wait_ge(sm["rank_i_done"], b.n + 1)
                v.tensor_scalar(tile_i[:], rank_i[:], 7, None, ALU.logical_shift_right).then_inc(sm["split_done"], 1)
                v.tensor_scalar(place_i[:], rank_i[:], P - 1, None, ALU.bitwise_and).then_inc(sm["split_done"], 1)
                dve.wait_ge(sm["split_done"], (b.n + 1) * 3)
                v.tensor_copy(place[:], place_i[:]).then_inc(sm["code_done"], 1)
                v.tensor_tensor(code[:], tile_i[:], e_code[:], ALU.add).then_inc(sm["code_done"], 1)
                dve.wait_ge(sm["code_done"], (b.n + 1) * 2)
                v.tensor_scalar(place_hot[:, bass.ds(b.n, 1)].rearrange("p o k -> p (o k)"), iota_row[:], place[:],
                                None, ALU.is_equal).then_inc(sm["hot_done"], 1)
                v.tensor_scalar(code_tok[:, bass.ds(b.n, 1)].rearrange("p o k -> p (o k)"), iota_row[:], code[:],
                                tok1[:, bass.ds(b.n, 1)], ALU.is_equal, ALU.mult).then_inc(sm["hot_done"], 1)

            def reciprocals(b):
                dve.wait_ge(sm["exp_done"], (b.n + 1) * NQ)
                v.reciprocal(recips[:], sums[:, b.p]).then_inc(sm["recip_done"], 1)
                dve.wait_ge(sm["recip_done"], b.n + 1)
                v.tensor_copy(recips_d[:], recips[:].unsqueeze(2).broadcast_to([P, HEADS, HD]))\
                    .then_inc(sm["recip_d_done"], 1)

            def normalize_heads(b):
                dve.wait_ge(sm["rT_taken"], b.n + 1)
                dve.wait_ge(sm["values_weighed"], (b.n + 1) * NQ)
                v.tensor_tensor(oT[:, b.p], BANK_A[:, 0:D].rearrange("p (c s) -> p c s", c=KC), recipsT[:],
                                ALU.mult).then_inc(sm["oT_done"], 1)

            def first():
                v.memset(mean_var[:], 1.0).then_inc(sm["consts_dve"], 1)
                dve.wait_ge(sm["consts_dve"], 1)
                dve.wait_ge(sm["consts_pool"], 3)
                dve.wait_ge(sm["bias_in"], 16 * 6)
                b = Batch(0, 0)
                stats_x(b)
                dve.wait_ge(sm["aggr1"], 1)
                inverse_roots(0)
                normalize(xn[:], x_sb[:, 0], LN1, sm["xn_done"])
                take_v(b)

            def step(b, nxt, prev):
                if nxt is not None:
                    stats_x(nxt)
                for q in range(NQ):
                    maxima(b, q)
                if prev is not None:
                    residual(prev)
                    dve.wait_ge(sm["aggr2"], prev.n + 1)
                if nxt is not None:
                    dve.wait_ge(sm["aggr1"], nxt.n + 1)
                inverse_roots(b.n + 1)
                if nxt is not None:
                    normalize(xn[:], x_sb[:, nxt.p], LN1, sm["xn_done"])
                if prev is not None:
                    normalize(record[:, prev.p, D:2 * D], record[:, prev.p, 0:D], LN2, sm["xn2_done"])
                if nxt is not None:
                    take_v(nxt)
                reciprocals(b)
                if prev is not None:
                    choose(prev)
                    place_tokens(prev)
                normalize_heads(b)

            def last(b):
                residual(b)
                dve.wait_ge(sm["aggr2"], b.n + 1)
                inverse_roots(b.n + 2)
                normalize(record[:, b.p, D:2 * D], record[:, b.p, 0:D], LN2, sm["xn2_done"])
                choose(b)
                place_tokens(b)

            steps(dve, first, step, last)

            n = [0]

            def link(ins):
                n[0] += 1
                ins.then_inc(sm["table"], 1)
                dve.wait_ge(sm["table"], n[0])

            dve.wait_ge(sm["total_ready"], 1)
            link(v.memset(ends[:], 0.0))
            link(v.tensor_scalar(n_i[:], BANK_A[:, 0:E], float(P - 1), None, ALU.add))
            link(v.tensor_scalar(n_sh[:], n_i[:], 7, None, ALU.logical_shift_right))
            link(v.tensor_copy(n_f[:], n_sh[:]))
            link(v.tensor_copy(ends[:, 0, PAD:], n_f[:]))
            for k, shift in enumerate((1, 2, 4)):
                link(v.tensor_tensor(ends[:, k + 1, PAD:], ends[:, k, PAD:],
                                     ends[:, k, PAD - shift:PAD + E - shift], ALU.add))
            by_slot = [P, SLOTS_W, E]
            link(v.tensor_tensor(passed[:], slot_f[:].unsqueeze(2).broadcast_to(by_slot),
                                 ends[:, 3, PAD:].unsqueeze(1).broadcast_to(by_slot), ALU.is_ge))
            link(v.tensor_tensor(passed_n[:], passed[:], n_f[:].unsqueeze(1).broadcast_to(by_slot), ALU.mult))
            link(v.tensor_reduce(slot_e[:], passed[:], AX_X, ALU.add))
            link(v.tensor_reduce(slot_start[:], passed_n[:], AX_X, ALU.add))
            v.tensor_scalar(slot_e_i[:], slot_e[:], float(E - 1), None, ALU.min).then_inc(sm["slots_done"], 1)
            link(v.tensor_tensor(slot_c[:], slot_f[:], slot_start[:], ALU.subtract))
            link(v.scalar_tensor_tensor(out=slot_code[:], in0=slot_e[:], scalar=float(TILES), in1=slot_c[:],
                                        op0=ALU.mult, op1=ALU.add))
            link(v.tensor_scalar(code_hot[:], slot_code[:], iota_part[:], None, ALU.is_equal))
            dve.wait_ge(sm["ids_T_ready"], 1)
            v.tensor_copy(ids_T[:], BANK_B[:, 0:P]).then_inc(sm["ids_T_done"], 1)
            dve.wait_ge(sm["ids_ready"], 1)
            link(v.tensor_copy(ids[:], BANK_A[:, 0:SLOTS_W]))
            link(v.tensor_scalar(ids_pad[:], ids[:], 0.0, float(OUT_OF_BOUNDS), ALU.is_equal, ALU.mult))
            v.tensor_scalar(gather_i[:], ids[:], -1.0, 0.0, ALU.add, ALU.max).then_inc(sm["index_done"], 1)
            v.scalar_tensor_tensor(out=scatter_i[:], in0=ids[:], scalar=-1.0, in1=ids_pad[:],
                                   op0=ALU.add, op1=ALU.add).then_inc(sm["index_done"], 1)

            with nc.vector.register("slot_expert_dve") as reg:
                def expert_copies(s, p, j):
                    for c in range(2):
                        dve.wait_ge(sm["h_ready"], s * 2 + (c + 1))
                        v.tensor_copy(h_sb[:, 512 * c:512 * (c + 1)], S_BANK[c][:]).then_inc(sm["h_taken"], 1)
                    v.reg_load(reg, slot_e_i[0:1, bass.ds(s, 1)])
                    e = nc.s_assert_within(v.snap(reg), 0, E - 1)
                    dve.wait_ge(gathered_in[p], (j + 1) * 16)
                    if isinstance(j, int) or True:
                        free_y(p, j)
                    v.tensor_tensor(y_sb[:, p], gathered[:, p, 0:D], b2_sb[:, bass.ds(e * D, D)], ALU.add)\
                        .then_inc(sm["b2_done"], 1)
                    dve.wait_ge(sm["b2_done"], s + 1)
                    dve.wait_ge(sm["ye_ready"], s + 1)
                    v.tensor_tensor(y_sb[:, p], y_sb[:, p], S_BANK[2 + p][:, 0:D], ALU.add)\
                        .then_inc(sm["ye_done"], 1)

                def free_y(p, j):
                    if isinstance(j, int) and j == 0:
                        return
                    dve.wait_ge(y_out[p], j * 16)

                dve.wait_ge(sm["slots_done"], 1)
                dve.wait_ge(sm["b2_in"], 16)
                expert_copies(0, 0, 0)
                expert_copies(1, 1, 0)
                with dve.Fori(1, SLOTS // 2) as j:
                    expert_copies(j * 2, 0, j)
                    expert_copies(j * 2 + 1, 1, j)
                if SLOTS % 2:
                    expert_copies(SLOTS - 1, 0, SLOTS // 2)

        @block.tensor
        def _(pe):
            t = nc.tensor

            def project_k(b):
                pe.wait_ge(ctx_in[b.p], (b.half + 1) * 16)
                for m in range(KC):
                    for c in range(KC):
                        ins = t.matmul(BANK_B[:, P * m:P * (m + 1)], wk_sb[:, c, P * m:P * (m + 1)], ctx_sb[:, b.p, c],
                                       start=(c == 0), stop=(c == KC - 1))
                ins.then_inc(sm["k_ready"], 1)

            def project_v(b):
                for c in range(KC):
                    ins = t.matmul(BANK_A[:, 0:D], ctx_sb[:, b.p, c], wv_sb[:, c], start=(c == 0), stop=(c == KC - 1))
                ins.then_inc(sm["v_ready"], 1)

            def turn_x(b):
                pe.wait_ge(sm["k_taken"], b.n + 1)
                pe.wait_ge(sm["xn_done"], b.n + 1)
                for c in range(KC):
                    ins = t.transpose(BANK_B[:, P * c:P * (c + 1)], xn[:, P * c:P * (c + 1)], ident[:])
                ins.then_inc(sm["xT_ready"], 1)

            def project_q(b):
                pe.wait_ge(sm["xT_taken"], b.n + 1)
                for m in range(KC):
                    for c in range(KC):
                        ins = t.matmul(BANK_B[:, P * m:P * (m + 1)], wq_sb[:, c, P * m:P * (m + 1)], xnT[:, c],
                                       start=(c == 0), stop=(c == KC - 1))
                ins.then_inc(sm["q_ready"], 1)

            def scores(b, first):
                pe.wait_ge(sm["q_taken"], b.n + 1)
                pe.wait_ge(kdiag_in[b.p], (b.half + 1) * (16 * KDIAG_DMAS))
                for q in range(NQ):
                    if not first:
                        pe.wait_ge(sm["exp_done"], b.n * NQ + (q + 1) - NQ)
                    c, h = q * QUAD // HG, q * QUAD % HG
                    t.matmul(S_BANK[q][:], qT[:, c], k_diag[:, c, h:h + QUAD].rearrange("p h k -> p (h k)"),
                             start=True, stop=True).then_inc(sm["scores_ready"], 1)

            def project_o(b):
                pe.wait_ge(sm["oT_done"], b.n + 1)
                for c in range(KC):
                    ins = t.matmul(BANK_A[:, 0:D], oT[:, b.p, c], wo_sb[:, c], start=(c == 0), stop=(c == KC - 1))
                ins.then_inc(sm["y_ready"], 1)

            def turn_x2(b):
                pe.wait_ge(sm["xn2_done"], b.n + 1)
                for c in range(KC):
                    ins = t.transpose(BANK_A[:, P * c:P * (c + 1)], record[:, b.p, D + P * c:D + P * (c + 1)], ident[:])
                ins.then_inc(sm["x2T_ready"], 1)

            def route(b):
                pe.wait_ge(sm["x2T_taken"], b.n + 1)
                for c in range(KC):
                    ins = t.matmul(BANK_B[:, 0:E], x2T[:, c], wr_sb[:, c], start=(c == 0), stop=(c == KC - 1))
                ins.then_inc(sm["logits_ready"], 1)

            def rank_tokens(b):
                pe.wait_ge(sm["onehot_done"], b.n + 1)
                t.matmul(BANK_B[:, 0:E], before[:], onehot[:, b.p], start=True, stop=False)
                if isinstance(b.n, int) and b.n == 0:
                    pass
                else:
                    pe.wait_ge(sm["seen_done"], b.n)
                t.matmul(BANK_B[:, 0:E], ones[:], seen[:], start=False, stop=True).then_inc(sm["rank_ready"], 1)

            def turn_probs(b, q):
                pe.wait_ge(sm["exp_done"], b.n * NQ + (q + 1))
                if not (isinstance(b.n, int) and b.n == 0 and q < 2):
                    pe.wait_ge(sm["probsT_taken"], b.n * NQ + q - 1)
                for i in range(QUAD):
                    ins = t.transpose(T_BANK[q % 2][:, P * i:P * (i + 1)], probs[:, QUAD * q + i], ident[:])
                ins.then_inc(sm["probsT_ready"], 1)

            def weigh_values(b, q):
                pe.wait_ge(sm["probsT_taken"], b.n * NQ + (q + 1))
                for i in range(QUAD):
                    c, h = divmod(q * QUAD + i, HG)
                    ins = t.matmul(BANK_A[:, P * c:P * (c + 1)], v_diag[:, b.p, c, h], probsT[:, q % 2, P * i:P * (i + 1)],
                                   start=(h == 0), stop=(h == HG - 1))
                ins.then_inc(sm["values_weighed"], 1)

            def turn_recips(b):
                pe.wait_ge(sm["recip_d_done"], b.n + 1)
                flat = recips_d[:].rearrange("p h d -> p (h d)")
                for c in range(KC):
                    ins = t.transpose(BANK_B[:, P * c:P * (c + 1)], flat[:, P * c:P * (c + 1)], ident[:])
                ins.then_inc(sm["rT_ready"], 1)

            def first():
                b = Batch(0, 0)
                pe.wait_ge(sm["consts_pool"], 3)
                pe.wait_ge(sm["wk_in"], 16)
                project_k(b)
                pe.wait_ge(sm["wv_in"], 16)
                project_v(b)
                turn_x(b)
                pe.wait_ge(sm["wq_in"], 16)
                project_q(b)
                pe.wait_ge(sm["wo_in"], 16)
                pe.wait_ge(sm["wr_in"], 16)

            def step(b, nxt, prev):
                scores(b, prev is None)
                if prev is not None:
                    project_o(prev)
                if nxt is not None:
                    if prev is not None:
                        pe.wait_ge(sm["rT_taken"], b.n)
                    project_k(nxt)
                    if prev is not None:
                        pe.wait_ge(sm["x1_done"], b.n)
                    else:
                        pe.wait_ge(sm["v_taken"], 1)
                    project_v(nxt)
                    turn_x(nxt)
                if prev is not None:
                    if nxt is not None:
                        pe.wait_ge(sm["v_taken"], nxt.n + 1)
                    turn_x2(prev)
                turn_probs(b, 0)
                if nxt is not None:
                    project_q(nxt)
                turn_probs(b, 1)
                pe.wait_ge(sm["v_taken"], b.n + 1)
                if prev is not None:
                    pe.wait_ge(sm["x2T_taken"], b.n)
                else:
                    pe.wait_ge(sm["v_taken"], nxt.n + 1)
                weigh_values(b, 0)
                if nxt is not None:
                    pe.wait_ge(sm["q_taken"], nxt.n + 1)
                if prev is not None:
                    route(prev)
                turn_probs(b, 2)
                weigh_values(b, 1)
                if prev is not None:
                    rank_tokens(prev)
                turn_probs(b, 3)
                weigh_values(b, 2)
                weigh_values(b, 3)
                if prev is not None:
                    pe.wait_ge(sm["ranked_done"], b.n)
                turn_recips(b)

            def last(b):
                project_o(b)
                turn_x2(b)
                pe.wait_ge(sm["rT_taken"], b.n + 1)
                route(b)
                rank_tokens(b)

            steps(pe, first, step, last)

            pe.wait_ge(sm["seen_done"], NB)
            t.matmul(BANK_A[:, 0:E], ones[:], seen[:], start=True, stop=True).then_inc(sm["total_ready"], 1)
            pe.wait_ge(sm["hot_done"], 2 * NB)
            for b in range(NB):
                ins = t.matmul(BANK_B[:, 0:P], code_tok[:, b], place_hot[:, b], start=(b == 0), stop=(b == NB - 1))
            ins.then_inc(sm["ids_T_ready"], 1)
            pe.wait_ge(sm["ids_T_done"], 1)
            pe.wait_ge(sm["slots_done"], 1)
            pe.wait_ge(sm["table"], 15)
            t.matmul(BANK_A[:, 0:SLOTS_W], ids_T[:], code_hot[:], start=True, stop=True).then_inc(sm["ids_ready"], 1)

            pe.wait_ge(sm["w1_in"], 16 * E)
            pe.wait_ge(sm["w2_in"], 16 * E)
            pe.wait_ge(sm["table"], 16)

            def up(s, p, j, e):
                pe.wait_ge(gathered_in[p], (j + 1) * 16)
                for c in range(KC):
                    ins = t.transpose(BANK_A[:, P * c:P * (c + 1)], gathered[:, p, D + P * c:D + P * (c + 1)], ident[:])
                ins.then_inc(sm["xeT_ready"], 1)
                pe.wait_ge(sm["xeT_taken"], s + 1)
                for n in range(2):
                    for c in range(KC):
                        ins = t.matmul(S_BANK[n][:], xeT[:, p, c],
                                       w1_flat[:, bass.ds(e * (KC * F) + (c * F + 512 * n), 512)],
                                       start=(c == 0), stop=(c == KC - 1))
                    ins.then_inc(sm["h_ready"], 1)

            def turn_h(s):
                for c in range(FC):
                    if c % 4 == 0:
                        pe.wait_ge(sm["h_taken"], s * 2 + (c // 4 + 1))
                    ins = t.transpose(T_BANK[c // 4][:, P * (c % 4):P * (c % 4 + 1)], h_sb[:, P * c:P * (c + 1)],
                                      ident[:])
                    if c % 4 == 3:
                        ins.then_inc(sm["hT_ready"], 1)

            def down(s, p, e):
                for c in range(FC):
                    if c % 4 == 0:
                        pe.wait_ge(sm["gelu_done"], s * 2 + (c // 4 + 1))
                    ins = t.matmul(S_BANK[2 + p][:, 0:D], hT[:, c],
                                   w2_flat[:, bass.ds(e * (FC * D) + c * D, D)],
                                   start=(c == 0), stop=(c == FC - 1))
                ins.then_inc(sm["ye_ready"], 1)

            w1_flat = w1_sb[:].rearrange("p e c f -> p (e c f)")
            w2_flat = w2_sb[:].rearrange("p e c d -> p (e c d)")
            with nc.tensor.register("slot_expert_0") as reg0, nc.tensor.register("slot_expert_1") as reg1:
                def expert_of(reg, s):
                    t.reg_load(reg, slot_e_i[0:1, bass.ds(s, 1)])
                    return nc.s_assert_within(t.snap(reg), 0, E - 1)

                e0 = expert_of(reg0, 0)
                up(0, 0, 0, e0)
                turn_h(0)
                with pe.Fori(0, (SLOTS - 1) // 2) as j:
                    s = j * 2
                    up(s + 1, 1, j, expert_of(reg1, s + 1))
                    down(s, 0, expert_of(reg0, s))
                    turn_h(s + 1)
                    up(s + 2, 0, j + 1, expert_of(reg0, s + 2))
                    down(s + 1, 1, expert_of(reg1, s + 1))
                    turn_h(s + 2)
                assert SLOTS % 2 == 1
                down(SLOTS - 1, 0, expert_of(reg0, SLOTS - 1))


def kernel(x, ctx_1024, L0_xattn_Wq, L0_xattn_bq, L0_xattn_Wk, L0_xattn_bk, L0_xattn_Wv, L0_xattn_bv, L0_xattn_Wo,
           L0_xattn_bo, L0_ffn_wr, L0_ffn_br, L0_ffn_w1, L0_ffn_b1, L0_ffn_w2, L0_ffn_b2):
    import numpy as np
    import concourse.bacc as bacc
    from concourse.bass_utils import run_bass_kernel_spmd as run

    x = np.asarray(x)
    E, F = np.asarray(L0_ffn_b1).shape
    arrays = {
        "x": x,
        "ctxT": np.asarray(ctx_1024).transpose(0, 2, 1),
        "wqT": np.asarray(L0_xattn_Wq).T, "bqT": np.asarray(L0_xattn_bq).reshape(-1, 128).T,
        "wkT": np.asarray(L0_xattn_Wk).T, "bkT": np.asarray(L0_xattn_bk).reshape(-1, 128).T,
        "wvT": np.asarray(L0_xattn_Wv).T, "bv": L0_xattn_bv,
        "woT": np.asarray(L0_xattn_Wo).T, "bo": L0_xattn_bo,
        "wr": L0_ffn_wr, "br": L0_ffn_br,
        "w1": L0_ffn_w1, "b1T": np.asarray(L0_ffn_b1).reshape(E * F // 128, 128).T,
        "w2": L0_ffn_w2, "b2": np.asarray(L0_ffn_b2).reshape(-1),
    }
    arrays = {k: np.ascontiguousarray(v) for k, v in arrays.items()}
    nc = bacc.Bacc("TRN2", target_bir_lowering=False, num_devices=1)
    args = [nc.dram_tensor(f"in_{k}", v.shape, F32, kind="ExternalInput").ap() for k, v in arrays.items()]
    out = nc.dram_tensor("out", [x.shape[0] * x.shape[1], x.shape[2]], F32, kind="ExternalOutput").ap()
    cross_attention_moe_kernel(nc, *args, out)
    r = run(nc, [{f"in_{k}": v for k, v in arrays.items()}], core_ids=[0])
    return r.results[0]["out"].reshape(x.shape)
```

```python
from contextlib import ExitStack

import concourse.bass as bass
from concourse import mybir

ALU = mybir.AluOpType
ACT = mybir.ActivationFunctionType
AX_X = mybir.AxisListType.X
F32 = mybir.dt.float32
F16 = mybir.dt.float16
I32 = mybir.dt.int32


class Batch:

    def __init__(self, half, parity):
        self.half, self.p, self.n = half, parity, half * 2 + parity


def cross_attention_moe_kernel(nc, x, ctxT, wqT, bqT, wkT, bkT, wvT, bv, woT, bo, wr, br, w1, b1T, w2, b2, out):
    NB, S, D = x.shape
    P = 128
    KC = D // P
    HEADS = 16
    HD = D // HEADS
    HG = P // HD
    QUAD = 4
    NQ = HEADS // QUAD
    E, _, F = w1.shape
    FC = F // P
    NTOK = NB * S
    TILES = NTOK // P
    SLOTS = (NTOK + E * (P - 1)) // P
    SLOTS_W = SLOTS + SLOTS % 2
    EPS = 1e-5
    SCALE = float(HD) ** -0.5
    NEWTON_STEPS = 3
    NEWTON_OPS = 3 + 3 * NEWTON_STEPS
    RSQRT_MAGIC = 0x5F3759DF
    OUT_OF_BOUNDS = 2 * NTOK
    SCAN = (NB - 1).bit_length()
    assert S == P and D == KC * P and E * TILES == P

    with ExitStack() as ctx:
        def sb(name, shape, dt=F32):
            return ctx.enter_context(nc.sbuf_tensor(name, shape, dt))

        def psum(name, shape, dt=F32):
            return ctx.enter_context(nc.psum_tensor(name, shape, dt))

        def sem(name):
            return ctx.enter_context(nc.semaphore(name))

        w1_sb = sb("w1_sb", [P, E, KC, F])
        w2_sb = sb("w2_sb", [P, E, FC, D])
        b1_sb = sb("b1_sb", [P, E * FC])
        wq_sb = sb("wq_sb", [P, KC, D])
        wk_sb = sb("wk_sb", [P, KC, D])
        wv_sb = sb("wv_sb", [P, KC, D])
        wo_sb = sb("wo_sb", [P, KC, D])
        wr_sb = sb("wr_sb", [P, KC, E])
        bq_sb = sb("bq_sb", [P, KC])
        bk_sb = sb("bk_sb", [P, KC])
        bv_sb = sb("bv_sb", [P, D])
        bo_sb = sb("bo_sb", [P, D])
        br_sb = sb("br_sb", [P, E])
        ident = sb("ident", [P, P])
        before = sb("before", [P, P], F16)
        ones = sb("ones", [P, P], F16)
        iota_i = sb("iota_i", [P, P], I32)
        iota_row = sb("iota_row", [P, P])
        iota_part_i = sb("iota_part_i", [P, 1], I32)
        iota_part = sb("iota_part", [P, 1])
        rev_i = sb("rev_i", [P, E], I32)
        rev = sb("rev", [P, E])
        tok_i = sb("tok_i", [P, NB], I32)
        tok1 = sb("tok1", [P, NB])

        x_sb = sb("x_sb", [P, 2, D])
        xb_sb = sb("xb_sb", [P, 2, D])
        ctx_sb = sb("ctx_sb", [P, 2, KC, P])
        xn = sb("xn", [P, D])
        xnT = sb("xnT", [P, KC, P])
        qT = sb("qT", [P, KC, P])
        kT = sb("kT", [P, KC, P])
        k_diag = sb("k_diag", [P, KC, HG, P])
        v_diag = sb("v_diag", [P, 2, KC, HG, P])
        probs = sb("probs", [P, HEADS, P])
        probsT = sb("probsT", [P, 2, QUAD * P])
        row_max = sb("row_max", [P, HEADS])
        neg_max = sb("neg_max", [P, HEADS])
        sums = sb("sums", [P, 2, HEADS])
        recips = sb("recips", [P, HEADS])
        recips_d = sb("recips_d", [P, HEADS, HD])
        recipsT = sb("recipsT", [P, KC, P])
        oT = sb("oT", [P, 2, KC, P])
        record = sb("record", [P, 2, 2 * D])
        x2T = sb("x2T", [P, KC, P])
        stats = sb("stats", [P, 2, 6])
        mean_var = sb("mean_var", [P, 2, 2])
        nw_y = sb("nw_y", [P, 2])
        nw_i = sb("nw_i", [P, 2], I32)
        nw_v = sb("nw_v", [P, 2])
        nw_t = sb("nw_t", [P, 2])
        nw_u = sb("nw_u", [P, 2])
        logits = sb("logits", [P, NB, E])
        best = sb("best", [P, NB])
        keyed = sb("keyed", [P, NB, E])
        key = sb("key", [P, NB])
        onehot = sb("onehot", [P, NB, E], F16)
        seen = sb("seen", [P, 2, NB + 1, E], F16)
        ranked = sb("ranked", [P, NB, E])
        rank, place, e_code, code = (sb(n, [P, NB]) for n in ("rank", "place", "e_code", "code"))
        rank_i, tile_i, place_i = (sb(n, [P, NB], I32) for n in ("rank_i", "tile_i", "place_i"))
        hots = probs[:].bitcast(F16).rearrange("p (o h) k -> p o (h k)", o=2)
        place_hot, code_tok = (hots[:, i].rearrange("p (b k) -> p b k", k=P) for i in range(2))

        PAD = E
        n_i = sb("n_i", [P, E], I32)
        n_sh = sb("n_sh", [P, E], I32)
        n_f = sb("n_f", [P, E])
        ends = sb("ends", [P, 4, PAD + E])
        slot_i = sb("slot_i", [P, SLOTS_W], I32)
        slot_f = sb("slot_f", [P, SLOTS_W])
        passed, passed_n = (probsT[:, i, 0:SLOTS_W * E].rearrange("p (s e) -> p s e", e=E) for i in range(2))
        slot_e = sb("slot_e", [P, SLOTS_W])
        slot_start = sb("slot_start", [P, SLOTS_W])
        slot_e_i = sb("slot_e_i", [P, SLOTS_W], I32)
        slot_c = sb("slot_c", [P, SLOTS_W])
        slot_code = sb("slot_code", [P, SLOTS_W])
        code_hot = sb("code_hot", [P, SLOTS_W], F16)
        ids_T = sb("ids_T", [P, P], F16)
        ids = sb("ids", [P, SLOTS_W])
        ids_pad = sb("ids_pad", [P, SLOTS_W])
        gather_i = sb("gather_i", [P, SLOTS_W], I32)
        scatter_i = sb("scatter_i", [P, SLOTS_W], I32)
        g_idx = sb("g_idx", [P, 2, 1], I32)
        s_idx = sb("s_idx", [P, 2, 1], I32)

        spare = v_diag[:].rearrange("p b c h s -> p (b c h s)")
        gathered = spare[:, 0:4 * D].rearrange("p (b d) -> p b d", b=2)
        xeT = spare[:, 4 * D:6 * D].rearrange("p (b c s) -> p b c s", b=2, c=KC)
        hT = spare[:, 6 * D:6 * D + F].rearrange("p (c s) -> p c s", c=FC)
        h_sb = probsT[:].rearrange("p b k -> p (b k)")
        y_sb = record[:, 0].rearrange("p (b d) -> p b d", b=2)
        x1_b2 = record[:, 1].rearrange("p (b d) -> p b d", b=2)
        b2_sb = k_diag[:].rearrange("p c h s -> p (c h s)")[:, 0:E * D]

        banks = [psum(f"bank{i}", [P, 512]) for i in range(8)]
        S_BANK, O_BANK, T_BANK = banks[0:3], banks[3], banks[4:6]
        Y_BANK = banks[2:4]
        BANK_A, BANK_B = banks[6], banks[7]

        records = nc.dram_tensor("records", [NTOK, 2 * D], F32).ap()

        names = """consts_pool consts_dve wq_in wk_in wv_in wo_in wr_in bias_in w1_in w2_in b2_in
            xb_done k_ready k_taken v_ready v_taken xT_ready xT_taken q_ready q_taken
            stats1 aggr1 stats2 aggr2 newton xn_done xn2_done scores_ready max_done neg_done exp_done
            probsT_ready probsT_taken values_weighed recip_done recip_d_done rT_ready rT_taken oT_done
            y_ready x1_done x2T_ready x2T_taken logits_ready logits_taken
            onehot_done rank_ready seen_done code_done hot_done total_ready table ids_T_ready ids_T_done
            ids_ready ids_taken index_done slots_done
            idx_copied scattered xeT_ready xeT_taken h_ready h_taken hT_ready gelu_done ye_ready ye_done
            b2_done""".split()
        sm = {n: sem(n) for n in names}
        x_in = [sem("x_in0"), sem("x_in1")]
        ctx_in = [sem("ctx_in0"), sem("ctx_in1")]
        kdiag_in = [sem("kdiag_in0"), sem("kdiag_in1")]
        record_out = [sem("record_out0"), sem("record_out1")]
        gathered_in = [sem("gathered_in0"), sem("gathered_in1")]
        y_out = [sem("y_out0"), sem("y_out1")]

        KDIAG_DMAS = HG

        def held(eng, value):
            return value if isinstance(value, int) else eng.to_reg(value)

        def steps(eng, first, step, last):
            first()
            step(Batch(0, 0), Batch(0, 1), Batch(1, 0), None)
            with eng.Fori(0, NB // 2 - 2) as j:
                step(Batch(j, 1), Batch(j + 1, 0), Batch(j + 1, 1), Batch(j, 0))
                step(Batch(j + 1, 0), Batch(j + 1, 1), Batch(j + 2, 0), Batch(j, 1))
            h = NB // 2 - 1
            step(Batch(h - 1, 1), Batch(h, 0), Batch(h, 1), Batch(h - 1, 0))
            step(Batch(h, 0), Batch(h, 1), None, Batch(h - 1, 1))
            step(Batch(h, 1), None, None, Batch(h, 0))
            last(Batch(h, 1))

        def slots(eng, body):
            assert SLOTS % 2 == 1
            body(0, 0, 0)
            with eng.Fori(0, SLOTS // 2) as j:
                body(j * 2 + 1, 1, j)
                body(j * 2 + 2, 0, j + 1)

        block = ctx.enter_context(nc.Block())

        @block.sync
        def _(sp):
            def load(b):
                sp.dma_start(ctx_sb[:, b.p], ctxT[bass.ds(b.n, 1)].rearrange("o (c p) s -> p (o c) s", p=P)).then_inc(ctx_in[b.p], 16)
                sp.dma_start(x_sb[:, b.p], x[bass.ds(b.n, 1)].rearrange("o p d -> p (o d)")).then_inc(x_in[b.p], 16)

            def k_blocks(b):
                taken, scored = held(sp, b.n + 1), held(sp, b.n * NQ)
                sp.wait_ge(sm["consts_pool"], 3)
                sp.wait_ge(sm["k_taken"], taken)
                if not (isinstance(b.n, int) and b.n == 0):
                    sp.wait_ge(sm["scores_ready"], scored)
                for h in range(HG):
                    rows = slice(HD * h, HD * (h + 1))
                    sp.dma_start(k_diag[rows, :, h, :], kT[rows]).then_inc(kdiag_in[b.p], 16)

            def save_record(b):
                sp.wait_ge(sm["xn2_done"], b.n + 1)
                sp.dma_start(records[bass.ds(b.n * P, P), :], record[:, b.p]).then_inc(record_out[b.p], 16)

            def first():
                for b, names in ((Batch(0, 0), (("wk_in", wk_sb, wkT), ("wv_in", wv_sb, wvT), ("wq_in", wq_sb, wqT))),
                                 (Batch(0, 1), (("wo_in", wo_sb, woT),))):
                    load(b)
                    for name, dst, src in names:
                        sp.dma_start(dst[:], src.rearrange("(c p) n -> p c n", p=P)).then_inc(sm[name], 16)
                sp.dma_start(wr_sb[:], wr.rearrange("(c p) e -> p c e", p=P)).then_inc(sm["wr_in"], 16)
                k_blocks(Batch(0, 0))

            def step(b, nxt, after, prev):
                if after is not None:
                    sp.wait_ge(sm["v_ready"], b.n + 1)
                    sp.wait_ge(sm["xn_done"], b.n + 1)
                    sp.wait_ge(sm["xb_done"], b.n + 1)
                    load(after)
                if nxt is not None:
                    k_blocks(nxt)
                if prev is not None:
                    save_record(prev)

            def last(b):
                save_record(b)
                sp.dma_start(b2_sb, b2.rearrange("(o n) -> o n", o=1).broadcast_to([P, E * D])).then_inc(sm["b2_in"], 16)

            steps(sp, first, step, last)

        @block.gpsimd
        def _(pool):
            g = nc.gpsimd
            g.memset(k_diag[:], 0.0)
            g.memset(v_diag[:], 0.0)
            g.memset(ident[:], 0.0)
            g.memset(before[:], 1.0)
            g.memset(ends[:], 0.0)
            g.memset(seen[:], 0.0).then_inc(sm["consts_pool"], 1)
            pool.wait_ge(sm["consts_pool"], 1)
            g.affine_select(out=ident[:], in_=ident[:], compare_op=ALU.not_equal, fill=1.0, base=0,
                            pattern=[[-1, P]], channel_multiplier=1)
            g.affine_select(out=before[:], in_=before[:], compare_op=ALU.is_ge, fill=0.0, base=-1,
                            pattern=[[1, P]], channel_multiplier=-1)
            g.memset(ones[:], 1.0)
            g.iota(iota_i[:], pattern=[[1, P]], base=0, channel_multiplier=0)
            g.iota(iota_part_i[:], pattern=[[1, 1]], base=0, channel_multiplier=1)
            g.iota(rev_i[:], pattern=[[-1, E]], base=E, channel_multiplier=0)
            g.iota(tok_i[:], pattern=[[P, NB]], base=1, channel_multiplier=1)
            g.iota(slot_i[:], pattern=[[1, SLOTS_W]], base=0, channel_multiplier=0).then_inc(sm["consts_pool"], 1)
            pool.wait_ge(sm["consts_pool"], 2)
            g.tensor_copy(iota_row[:], iota_i[:])
            g.tensor_copy(iota_part[:], iota_part_i[:])
            g.tensor_copy(rev[:], rev_i[:])
            g.tensor_copy(tok1[:], tok_i[:])
            g.tensor_copy(slot_f[:], slot_i[:]).then_inc(sm["consts_pool"], 1)

            def add_bo(b, used):
                pool.wait_ge(x_in[b.p], (b.half + 1) * 16)
                if used is not None:
                    pool.wait_ge(sm["x1_done"], used.n + 1)
                g.tensor_tensor(xb_sb[:, b.p], x_sb[:, b.p], bo_sb[:], ALU.add).then_inc(sm["xb_done"], 1)

            pool.wait_ge(sm["bias_in"], 16 * 6)
            add_bo(Batch(0, 0), None)
            add_bo(Batch(0, 1), None)
            with pool.Fori(0, NB // 2 - 1) as j:
                add_bo(Batch(j + 1, 0), Batch(j, 0))
                add_bo(Batch(j + 1, 1), Batch(j, 1))

            def scatter(s, p, j):
                if not (isinstance(j, int) and j == 0):
                    pool.wait_ge(y_out[p], j * 16)
                g.tensor_copy(s_idx[:, p], scatter_i[:, bass.ds(s, 1)]).then_inc(sm["scattered"], 1)
                count = held(pool, s + 1)
                pool.wait_ge(sm["index_done"], 2)
                pool.wait_ge(sm["scattered"], count)
                pool.wait_ge(sm["ye_done"], count)
                g.indirect_dma_start(out=out[:, :], out_offset=bass.IndirectOffsetOnAxis(ap=s_idx[:, p], axis=0),
                                     in_=y_sb[:, p], in_offset=None, bounds_check=NTOK - 1, oob_is_err=False)\
                    .then_inc(y_out[p], 16)

            def gather(s, p, wait_used=True):
                if wait_used:
                    pool.wait_ge(sm["b2_done"], s - 1)
                    pool.wait_ge(sm["xeT_taken"], s - 1)
                g.tensor_copy(g_idx[:, p], gather_i[:, bass.ds(s, 1)]).then_inc(sm["idx_copied"], 1)
                copied = held(pool, s + 1)
                pool.wait_ge(sm["index_done"], 2)
                pool.wait_ge(sm["idx_copied"], copied)
                g.indirect_dma_start(out=gathered[:, p], out_offset=None, in_=records[:, :],
                                     in_offset=bass.IndirectOffsetOnAxis(ap=g_idx[:, p], axis=0))\
                    .then_inc(gathered_in[p], 16)

            pool.wait_ge(sm["index_done"], 2)
            for p in range(2):
                pool.wait_ge(record_out[p], 16 * (NB // 2))
            gather(0, 0, False)
            gather(1, 1, False)
            gather(2, 0)
            scatter(0, 0, 0)
            gather(3, 1)
            scatter(1, 1, 0)
            with pool.Fori(1, (SLOTS - 2) // 2) as j:
                gather(j * 2 + 2, 0)
                scatter(j * 2, 0, j)
                gather(j * 2 + 3, 1)
                scatter(j * 2 + 1, 1, j)
            done = (SLOTS - 2) // 2 * 2
            for s in range(done, SLOTS):
                if s + 2 < SLOTS:
                    gather(s + 2, s % 2)
                scatter(s, s % 2, s // 2)
            pool.wait_ge(y_out[0], 16 * ((SLOTS + 1) // 2))
            pool.wait_ge(y_out[1], 16 * (SLOTS // 2))

        @block.scalar
        def _(act):
            a = nc.scalar

            def rep(v, n):
                return v.rearrange("(o n) -> o n", o=1).broadcast_to([P, n])

            act.dma_start(bk_sb[:], bkT).then_inc(sm["bias_in"], 16)
            act.dma_start(bq_sb[:], bqT).then_inc(sm["bias_in"], 16)
            act.dma_start(bv_sb[:], rep(bv, D)).then_inc(sm["bias_in"], 16)
            act.dma_start(bo_sb[:], rep(bo, D)).then_inc(sm["bias_in"], 16)
            act.dma_start(br_sb[:], rep(br, E)).then_inc(sm["bias_in"], 16)
            act.dma_start(b1_sb[:], b1T).then_inc(sm["bias_in"], 16)

            def load_expert(b):
                e = bass.ds(b.half, 1)
                if b.p == 0:
                    act.dma_start(w1_sb[:, e].rearrange("p o c f -> p (o c) f"),
                                  w1[e].rearrange("o (c p) f -> p (o c) f", p=P)).then_inc(sm["w1_in"], 16)
                else:
                    act.dma_start(w2_sb[:, e].rearrange("p o c d -> p (o c) d"),
                                  w2[e].rearrange("o (c p) d -> p (o c) d", p=P)).then_inc(sm["w2_in"], 16)

            def exps(b, q):
                act.wait_ge(sm["neg_done"], b.n * NQ + (q + 1))
                for i in range(QUAD):
                    h = QUAD * q + i
                    ins = a.activation(probs[:, h], S_BANK[q % 3][:, P * i:P * (i + 1)], ACT.Exp, scale=SCALE,
                                       bias=neg_max[:, h:h + 1], accum_out=sums[:, b.p, h:h + 1])
                ins.then_inc(sm["exp_done"], 1)

            def take_k(b, prev):
                act.wait_ge(sm["k_ready"], b.n + 1)
                if prev is not None:
                    act.wait_ge(kdiag_in[prev.p], (prev.half + 1) * (16 * KDIAG_DMAS))
                for c in range(KC):
                    ins = a.activation(kT[:, c], BANK_B[:, P * c:P * (c + 1)], ACT.Identity,
                                       bias=bk_sb[:, c:c + 1])
                ins.then_inc(sm["k_taken"], 1)

            def take_xT(b):
                act.wait_ge(sm["xT_ready"], b.n + 1)
                a.copy(xnT[:], BANK_A[:, 0:D].rearrange("p (c s) -> p c s", c=KC)).then_inc(sm["xT_taken"], 1)

            def take_q(b):
                act.wait_ge(sm["q_ready"], b.n + 1)
                for c in range(KC):
                    ins = a.activation(qT[:, c], BANK_A[:, P * c:P * (c + 1)], ACT.Identity,
                                       bias=bq_sb[:, c:c + 1])
                ins.then_inc(sm["q_taken"], 1)

            def take_x2T(b):
                act.wait_ge(sm["x2T_ready"], b.n + 1)
                a.copy(x2T[:], BANK_B[:, 0:D].rearrange("p (c s) -> p c s", c=KC)).then_inc(sm["x2T_taken"], 1)

            def take_probsT(b, q):
                act.wait_ge(sm["probsT_ready"], b.n * NQ + (q + 1))
                if q >= 2:
                    act.wait_ge(sm["values_weighed"], b.n * NQ + (q - 1))
                elif not (isinstance(b.n, int) and b.n == 0):
                    act.wait_ge(sm["values_weighed"], b.n * NQ + (q - 1))
                a.copy(probsT[:, q % 2], T_BANK[q % 2][:]).then_inc(sm["probsT_taken"], 1)

            def take_rT(b):
                act.wait_ge(sm["rT_ready"], b.n + 1)
                a.copy(recipsT[:], O_BANK[:, D:2 * D].rearrange("p (c s) -> p c s", c=KC)).then_inc(sm["rT_taken"], 1)

            def first():
                act.wait_ge(sm["bias_in"], 16 * 6)
                take_k(Batch(0, 0), None)
                take_xT(Batch(0, 0))
                take_q(Batch(0, 0))

            def step(b, nxt, after, prev):
                load_expert(b)
                for q in range(NQ - 1):
                    exps(b, q)
                if nxt is not None:
                    take_k(nxt, b)
                take_probsT(b, 0)
                if nxt is not None:
                    take_xT(nxt)
                exps(b, NQ - 1)
                take_probsT(b, 1)
                if nxt is not None:
                    take_q(nxt)
                take_probsT(b, 2)
                if prev is not None:
                    take_x2T(prev)
                take_probsT(b, 3)
                take_rT(b)

            def last(b):
                take_x2T(b)

            steps(act, first, step, last)

            with nc.scalar.register("slot_expert_act") as reg:
                def expert_gelu(s, p, j):
                    a.reg_load(reg, slot_e_i[0:1, bass.ds(s, 1)])
                    e = nc.s_assert_within(a.snap(reg), 0, E - 1)
                    for c in range(FC):
                        if c % 4 == 0:
                            act.wait_ge(sm["hT_ready"], s * 2 + (c // 4 + 1))
                        ins = a.activation(hT[:, c], T_BANK[c // 4][:, P * (c % 4):P * (c % 4 + 1)], ACT.Gelu,
                                           bias=b1_sb[:, bass.ds(e * FC + c, 1)])
                        if c % 4 == 3:
                            ins.then_inc(sm["gelu_done"], 1)
                act.wait_ge(sm["slots_done"], 1)
                slots(act, expert_gelu)

        @block.vector
        def _(dve):
            v = nc.vector
            LN2, LN1 = 0, 1

            def stats_of(src, col, name, count):
                count = held(dve, count)
                v.bn_stats(stats[:, col], src).then_inc(sm["stats" + name], 1)
                dve.wait_ge(sm["consts_dve"], 1)
                dve.wait_ge(sm["stats" + name], count)
                v.bn_aggr(mean_var[:, col], stats[:, col]).then_inc(sm["aggr" + name], 1)

            def stats_x(b):
                dve.wait_ge(x_in[b.p], (b.half + 1) * 16)
                if not isinstance(b.n, int) or b.n > 0:
                    dve.wait_ge(sm["xn_done"], b.n)
                stats_of(x_sb[:, b.p], LN1, "1", b.n + 1)

            def inverse_roots(turn):
                n = [0]

                def link(ins):
                    n[0] += 1
                    ins.then_inc(sm["newton"], 1)
                    dve.wait_ge(sm["newton"], turn * NEWTON_OPS + n[0])

                link(v.tensor_scalar(nw_v[:], mean_var[:, :, 1], EPS, None, ALU.add))
                link(v.tensor_scalar(nw_i[:], nw_v[:].bitcast(I32), 1, None, ALU.logical_shift_right))
                link(v.tensor_scalar(nw_y[:].bitcast(I32), nw_i[:], -1, RSQRT_MAGIC, ALU.mult, ALU.add))
                for _ in range(NEWTON_STEPS):
                    link(v.tensor_tensor(nw_t[:], nw_y[:], nw_y[:], ALU.mult))
                    link(v.scalar_tensor_tensor(out=nw_u[:], in0=nw_t[:], scalar=-0.5, in1=nw_v[:],
                                                op0=ALU.mult, op1=ALU.mult))
                    link(v.scalar_tensor_tensor(out=nw_y[:], in0=nw_u[:], scalar=1.5, in1=nw_y[:],
                                                op0=ALU.add, op1=ALU.mult))

            def normalize(dst, src, col, done):
                v.tensor_scalar(dst, src, mean_var[:, col, 0:1], nw_y[:, col:col + 1],
                                ALU.subtract, ALU.mult).then_inc(done, 1)

            def maxima(b, q):
                dve.wait_ge(sm["scores_ready"], b.n * NQ + (q + 1))
                hs = slice(QUAD * q, QUAD * (q + 1))
                v.tensor_reduce(row_max[:, hs], S_BANK[q % 3][:].rearrange("p (h k) -> p h k", k=P), AX_X,
                                ALU.max).then_inc(sm["max_done"], 1)
                dve.wait_ge(sm["max_done"], b.n * NQ + (q + 1))
                v.tensor_scalar(neg_max[:, hs], row_max[:, hs], -SCALE, None, ALU.mult).then_inc(sm["neg_done"], 1)

            def residual(b):
                dve.wait_ge(sm["y_ready"], b.n + 1)
                dve.wait_ge(sm["xb_done"], b.n + 1)
                if not isinstance(b.n, int) or b.n >= 2:
                    if isinstance(b.n, int):
                        dve.wait_ge(record_out[b.p], b.half * 16)
                    else:
                        dve.wait_ge(record_out[b.p], b.half * 16)
                v.tensor_tensor(record[:, b.p, 0:D], BANK_A[:, 0:D], xb_sb[:, b.p], ALU.add)\
                    .then_inc(sm["x1_done"], 1)
                dve.wait_ge(sm["x1_done"], b.n + 1)
                stats_of(record[:, b.p, 0:D], LN2, "2", b.n + 1)

            def take_v(b):
                dve.wait_ge(sm["v_ready"], b.n + 1)
                for c in range(KC):
                    blocks = v_diag[:, b.p, c].rearrange("p h (i d) -> p (h i) d", d=HD)[:, ::HG + 1, :]
                    ins = v.tensor_tensor(blocks, BANK_B[:, P * c:P * (c + 1)].rearrange("p (h d) -> p h d", d=HD),
                                          bv_sb[:, P * c:P * (c + 1)].rearrange("p (h d) -> p h d", d=HD), ALU.add)
                ins.then_inc(sm["v_taken"], 1)

            def take_logits(b):
                dve.wait_ge(sm["logits_ready"], b.n + 1)
                v.tensor_tensor(logits[:, bass.ds(b.n, 1)].rearrange("p o e -> p (o e)"), BANK_A[:, 0:E], br_sb[:],
                                ALU.add).then_inc(sm["logits_taken"], 1)

            def reciprocals(b):
                dve.wait_ge(sm["exp_done"], (b.n + 1) * NQ)
                v.reciprocal(recips[:], sums[:, b.p]).then_inc(sm["recip_done"], 1)
                dve.wait_ge(sm["recip_done"], b.n + 1)
                v.tensor_copy(recips_d[:], recips[:].unsqueeze(2).broadcast_to([P, HEADS, HD]))\
                    .then_inc(sm["recip_d_done"], 1)

            def normalize_heads(b):
                dve.wait_ge(sm["rT_taken"], b.n + 1)
                dve.wait_ge(sm["values_weighed"], (b.n + 1) * NQ)
                v.tensor_tensor(oT[:, b.p], O_BANK[:, 0:D].rearrange("p (c s) -> p c s", c=KC), recipsT[:],
                                ALU.mult).then_inc(sm["oT_done"], 1)

            def first():
                v.memset(mean_var[:], 1.0).then_inc(sm["consts_dve"], 1)
                dve.wait_ge(sm["consts_dve"], 1)
                dve.wait_ge(sm["consts_pool"], 3)
                dve.wait_ge(sm["bias_in"], 16 * 6)
                b = Batch(0, 0)
                stats_x(b)
                dve.wait_ge(sm["aggr1"], 1)
                inverse_roots(0)
                normalize(xn[:], x_sb[:, 0], LN1, sm["xn_done"])
                take_v(b)
                stats_x(Batch(0, 1))
                dve.wait_ge(sm["aggr1"], 2)
                inverse_roots(1)

            def step(b, nxt, after, prev):
                if nxt is not None:
                    dve.wait_ge(sm["xT_ready"], b.n + 1)
                    normalize(xn[:], x_sb[:, nxt.p], LN1, sm["xn_done"])
                for q in range(NQ - 1):
                    maxima(b, q)
                if prev is not None:
                    residual(prev)
                maxima(b, NQ - 1)
                if after is not None:
                    stats_x(after)
                    dve.wait_ge(sm["aggr1"], after.n + 1)
                if prev is not None:
                    dve.wait_ge(sm["aggr2"], prev.n + 1)
                inverse_roots(b.n + 2)
                if nxt is not None:
                    take_v(nxt)
                if prev is not None:
                    normalize(record[:, prev.p, D:2 * D], record[:, prev.p, 0:D], LN2, sm["xn2_done"])
                reciprocals(b)
                if prev is not None:
                    take_logits(prev)
                normalize_heads(b)

            def last(b):
                residual(b)
                dve.wait_ge(sm["aggr2"], b.n + 1)
                inverse_roots(b.n + 3)
                normalize(record[:, b.p, D:2 * D], record[:, b.p, 0:D], LN2, sm["xn2_done"])
                take_logits(b)

            steps(dve, first, step, last)

            n = [0]

            def link(ins):
                n[0] += 1
                ins.then_inc(sm["table"], 1)
                dve.wait_ge(sm["table"], n[0])

            by_expert, by_place = [P, NB, E], [P, NB, P]
            dve.wait_ge(sm["logits_taken"], NB)
            link(v.tensor_reduce(best[:], logits[:], AX_X, ALU.max))
            link(v.tensor_tensor(keyed[:], logits[:], best[:].unsqueeze(2).broadcast_to(by_expert), ALU.is_equal))
            link(v.tensor_tensor(keyed[:], keyed[:], rev[:].unsqueeze(1).broadcast_to(by_expert), ALU.mult))
            link(v.tensor_reduce(key[:], keyed[:], AX_X, ALU.max))
            v.tensor_tensor(onehot[:], keyed[:], key[:].unsqueeze(2).broadcast_to(by_expert), ALU.is_equal)\
                .then_inc(sm["onehot_done"], 1)
            dve.wait_ge(sm["onehot_done"], 1)
            link(v.tensor_copy(seen[:, 0, 1:], onehot[:]))
            for k in range(SCAN):
                d = 1 << k
                link(v.tensor_tensor(seen[:, (k + 1) % 2, 1 + d:], seen[:, k % 2, 1 + d:],
                                     seen[:, k % 2, 1:NB + 1 - d], ALU.add))
                if k == SCAN - 1:
                    v.tensor_copy(seen[:, (k + 1) % 2, 1:1 + d], seen[:, k % 2, 1:1 + d]).then_inc(sm["seen_done"], 1)
                else:
                    link(v.tensor_copy(seen[:, (k + 1) % 2, 1:1 + d], seen[:, k % 2, 1:1 + d]))
            link(v.tensor_scalar(e_code[:], key[:], -float(TILES), float(E * TILES), ALU.mult, ALU.add))
            dve.wait_ge(sm["rank_ready"], 1)
            link(v.tensor_tensor(ranked[:], BANK_B[:, 0:NB * E].rearrange("p (b e) -> p b e", e=E), onehot[:], ALU.mult))
            link(v.tensor_reduce(rank[:], ranked[:], AX_X, ALU.add))
            link(v.tensor_copy(rank_i[:], rank[:]))
            link(v.tensor_scalar(tile_i[:], rank_i[:], 7, None, ALU.logical_shift_right))
            link(v.tensor_scalar(place_i[:], rank_i[:], P - 1, None, ALU.bitwise_and))
            link(v.tensor_copy(place[:], place_i[:]))
            link(v.tensor_tensor(code[:], tile_i[:], e_code[:], ALU.add))
            for b in range(NB):
                v.tensor_scalar(place_hot[:, b], iota_row[:], place[:, b:b + 1], None, ALU.is_equal)\
                    .then_inc(sm["hot_done"], 1)
                v.tensor_scalar(code_tok[:, b], iota_row[:], code[:, b:b + 1], tok1[:, b:b + 1], ALU.is_equal,
                                ALU.mult).then_inc(sm["hot_done"], 1)

            dve.wait_ge(sm["total_ready"], 1)
            link(v.tensor_scalar(n_i[:], BANK_A[:, 0:E], float(P - 1), None, ALU.add))
            link(v.tensor_scalar(n_sh[:], n_i[:], 7, None, ALU.logical_shift_right))
            link(v.tensor_copy(n_f[:], n_sh[:]))
            link(v.tensor_copy(ends[:, 0, PAD:], n_f[:]))
            for k, shift in enumerate((1, 2, 4)):
                link(v.tensor_tensor(ends[:, k + 1, PAD:], ends[:, k, PAD:],
                                     ends[:, k, PAD - shift:PAD + E - shift], ALU.add))
            by_slot = [P, SLOTS_W, E]
            link(v.tensor_tensor(passed[:], slot_f[:].unsqueeze(2).broadcast_to(by_slot),
                                 ends[:, 3, PAD:].unsqueeze(1).broadcast_to(by_slot), ALU.is_ge))
            link(v.tensor_tensor(passed_n[:], passed[:], n_f[:].unsqueeze(1).broadcast_to(by_slot), ALU.mult))
            link(v.tensor_reduce(slot_e[:], passed[:], AX_X, ALU.add))
            link(v.tensor_reduce(slot_start[:], passed_n[:], AX_X, ALU.add))
            v.tensor_scalar(slot_e_i[:], slot_e[:], float(E - 1), None, ALU.min).then_inc(sm["slots_done"], 1)
            link(v.tensor_tensor(slot_c[:], slot_f[:], slot_start[:], ALU.subtract))
            link(v.scalar_tensor_tensor(out=slot_code[:], in0=slot_e[:], scalar=float(TILES), in1=slot_c[:],
                                        op0=ALU.mult, op1=ALU.add))
            v.tensor_scalar(code_hot[:], slot_code[:], iota_part[:], None, ALU.is_equal).then_inc(sm["code_done"], 1)
            dve.wait_ge(sm["ids_T_ready"], 1)
            v.tensor_copy(ids_T[:], BANK_B[:, 0:P]).then_inc(sm["ids_T_done"], 1)
            dve.wait_ge(sm["ids_ready"], 1)
            v.tensor_copy(ids[:], BANK_A[:, 0:SLOTS_W]).then_inc(sm["ids_taken"], 1)
            dve.wait_ge(sm["ids_taken"], 1)
            v.tensor_scalar(gather_i[:], ids[:], -1.0, 0.0, ALU.add, ALU.max).then_inc(sm["index_done"], 1)
            link(v.tensor_scalar(ids_pad[:], ids[:], 0.0, float(OUT_OF_BOUNDS), ALU.is_equal, ALU.mult))
            v.scalar_tensor_tensor(out=scatter_i[:], in0=ids[:], scalar=-1.0, in1=ids_pad[:],
                                   op0=ALU.add, op1=ALU.add).then_inc(sm["index_done"], 1)

            with nc.vector.register("slot_expert_dve") as reg:
                def take_xe(s, p):
                    dve.wait_ge(sm["xeT_ready"], s + 1)
                    v.tensor_copy(xeT[:, p], BANK_A[:, 0:D].rearrange("p (c s) -> p c s", c=KC))\
                        .then_inc(sm["xeT_taken"], 1)

                def take_h(s):
                    for c in range(2):
                        dve.wait_ge(sm["h_ready"], s * 2 + (c + 1))
                        v.tensor_copy(h_sb[:, 512 * c:512 * (c + 1)], S_BANK[c][:]).then_inc(sm["h_taken"], 1)

                def add_b2(s, p, j):
                    v.reg_load(reg, slot_e_i[0:1, bass.ds(s, 1)])
                    e = nc.s_assert_within(v.snap(reg), 0, E - 1)
                    dve.wait_ge(gathered_in[p], (j + 1) * 16)
                    v.tensor_tensor(x1_b2[:, p], gathered[:, p, 0:D], b2_sb[:, bass.ds(e * D, D)], ALU.add)\
                        .then_inc(sm["b2_done"], 1)

                def finish(s, p, j):
                    dve.wait_ge(sm["b2_done"], s + 1)
                    dve.wait_ge(sm["ye_ready"], s + 1)
                    if not (isinstance(j, int) and j == 0):
                        dve.wait_ge(y_out[p], j * 16)
                    v.tensor_tensor(y_sb[:, p], x1_b2[:, p], Y_BANK[p][:, 0:D], ALU.add)\
                        .then_inc(sm["ye_done"], 1)

                def turn(s, p, j, more=True):
                    take_h(s + 1)
                    finish(s, p, j)
                    if more:
                        take_xe(s + 2, p)
                        dve.wait_ge(sm["ye_done"], s + 1)
                        add_b2(s + 2, p, j + 1)

                dve.wait_ge(sm["b2_in"], 16)
                for s in range(2):
                    take_xe(s, s)
                    add_b2(s, s, 0)
                take_h(0)
                turn(0, 0, 0)
                turn(1, 1, 0)
                with dve.Fori(1, SLOTS // 2 - 1) as j:
                    turn(j * 2, 0, j)
                    turn(j * 2 + 1, 1, j)
                j = SLOTS // 2 - 1
                turn(j * 2, 0, j)
                turn(j * 2 + 1, 1, j, False)
                finish(SLOTS - 1, 0, j + 1)

        @block.tensor
        def _(pe):
            t = nc.tensor

            def project_k(b):
                pe.wait_ge(ctx_in[b.p], (b.half + 1) * 16)
                for m in range(KC):
                    for c in range(KC):
                        ins = t.matmul(BANK_B[:, P * m:P * (m + 1)], wk_sb[:, c, P * m:P * (m + 1)], ctx_sb[:, b.p, c],
                                       start=(c == 0), stop=(c == KC - 1))
                ins.then_inc(sm["k_ready"], 1)

            def project_v(b):
                for c in range(KC):
                    ins = t.matmul(BANK_B[:, 0:D], ctx_sb[:, b.p, c], wv_sb[:, c], start=(c == 0), stop=(c == KC - 1))
                ins.then_inc(sm["v_ready"], 1)

            def turn_x(b):
                pe.wait_ge(sm["xn_done"], b.n + 1)
                for c in range(KC):
                    ins = t.transpose(BANK_A[:, P * c:P * (c + 1)], xn[:, P * c:P * (c + 1)], ident[:])
                ins.then_inc(sm["xT_ready"], 1)

            def project_q(b):
                pe.wait_ge(sm["xT_taken"], b.n + 1)
                for m in range(KC):
                    for c in range(KC):
                        ins = t.matmul(BANK_A[:, P * m:P * (m + 1)], wq_sb[:, c, P * m:P * (m + 1)], xnT[:, c],
                                       start=(c == 0), stop=(c == KC - 1))
                ins.then_inc(sm["q_ready"], 1)

            def scores(b, qs, first):
                if qs[0] == 0:
                    pe.wait_ge(sm["q_taken"], b.n + 1)
                    pe.wait_ge(kdiag_in[b.p], (b.half + 1) * (16 * KDIAG_DMAS))
                for q in qs:
                    if q == NQ - 1:
                        pe.wait_ge(sm["exp_done"], b.n * NQ + 1)
                    elif q == 0 and not first:
                        pe.wait_ge(sm["exp_done"], b.n * NQ)
                    c, h = q * QUAD // HG, q * QUAD % HG
                    t.matmul(S_BANK[q % 3][:], qT[:, c], k_diag[:, c, h:h + QUAD].rearrange("p h k -> p (h k)"),
                             start=True, stop=True).then_inc(sm["scores_ready"], 1)

            def project_o(b):
                pe.wait_ge(sm["oT_done"], b.n + 1)
                for c in range(KC):
                    ins = t.matmul(BANK_A[:, 0:D], oT[:, b.p, c], wo_sb[:, c], start=(c == 0), stop=(c == KC - 1))
                ins.then_inc(sm["y_ready"], 1)

            def turn_x2(b):
                pe.wait_ge(sm["xn2_done"], b.n + 1)
                for c in range(KC):
                    ins = t.transpose(BANK_B[:, P * c:P * (c + 1)], record[:, b.p, D + P * c:D + P * (c + 1)], ident[:])
                ins.then_inc(sm["x2T_ready"], 1)

            def route(b):
                pe.wait_ge(sm["x2T_taken"], b.n + 1)
                for c in range(KC):
                    ins = t.matmul(BANK_A[:, 0:E], x2T[:, c], wr_sb[:, c], start=(c == 0), stop=(c == KC - 1))
                ins.then_inc(sm["logits_ready"], 1)

            def turn_probs(b, q):
                pe.wait_ge(sm["exp_done"], b.n * NQ + (q + 1))
                if not (isinstance(b.n, int) and b.n == 0 and q < 2):
                    pe.wait_ge(sm["probsT_taken"], b.n * NQ + q - 1)
                for i in range(QUAD):
                    ins = t.transpose(T_BANK[q % 2][:, P * i:P * (i + 1)], probs[:, QUAD * q + i], ident[:])
                ins.then_inc(sm["probsT_ready"], 1)

            def weigh_values(b, q):
                pe.wait_ge(sm["probsT_taken"], b.n * NQ + (q + 1))
                for i in range(QUAD):
                    c, h = divmod(q * QUAD + i, HG)
                    ins = t.matmul(O_BANK[:, P * c:P * (c + 1)], v_diag[:, b.p, c, h], probsT[:, q % 2, P * i:P * (i + 1)],
                                   start=(h == 0), stop=(h == HG - 1))
                ins.then_inc(sm["values_weighed"], 1)

            def turn_recips(b):
                pe.wait_ge(sm["recip_d_done"], b.n + 1)
                flat = recips_d[:].rearrange("p h d -> p (h d)")
                for c in range(KC):
                    ins = t.transpose(O_BANK[:, D + P * c:D + P * (c + 1)], flat[:, P * c:P * (c + 1)], ident[:])
                ins.then_inc(sm["rT_ready"], 1)

            def first():
                b = Batch(0, 0)
                pe.wait_ge(sm["consts_pool"], 3)
                pe.wait_ge(sm["wk_in"], 16)
                project_k(b)
                turn_x(b)
                pe.wait_ge(sm["k_taken"], 1)
                pe.wait_ge(sm["wv_in"], 16)
                project_v(b)
                pe.wait_ge(sm["wq_in"], 16)
                project_q(b)
                pe.wait_ge(sm["v_taken"], 1)
                pe.wait_ge(sm["wo_in"], 16)
                pe.wait_ge(sm["wr_in"], 16)

            def step(b, nxt, after, prev):
                scores(b, range(NQ - 1), prev is None)
                if prev is not None:
                    pe.wait_ge(sm["oT_done"], b.n)
                    if not (isinstance(b.n, int) and b.n < 2):
                        pe.wait_ge(sm["logits_taken"], b.n - 1)
                    project_o(prev)
                scores(b, [NQ - 1], prev is None)
                if nxt is not None:
                    if prev is not None and not (isinstance(b.n, int) and b.n < 2):
                        pe.wait_ge(sm["x2T_taken"], b.n - 1)
                    project_k(nxt)
                turn_probs(b, 0)
                if nxt is not None:
                    if prev is not None:
                        pe.wait_ge(sm["x1_done"], b.n)
                    turn_x(nxt)
                turn_probs(b, 1)
                if nxt is not None:
                    pe.wait_ge(sm["k_taken"], nxt.n + 1)
                    project_v(nxt)
                weigh_values(b, 0)
                if nxt is not None:
                    project_q(nxt)
                turn_probs(b, 2)
                weigh_values(b, 1)
                if prev is not None:
                    if nxt is not None:
                        pe.wait_ge(sm["v_taken"], nxt.n + 1)
                    turn_x2(prev)
                turn_probs(b, 3)
                weigh_values(b, 2)
                if prev is not None:
                    if nxt is not None:
                        pe.wait_ge(sm["q_taken"], nxt.n + 1)
                    else:
                        pe.wait_ge(sm["x1_done"], b.n)
                    route(prev)
                weigh_values(b, 3)
                turn_recips(b)

            def last(b):
                pe.wait_ge(sm["logits_taken"], b.n)
                project_o(b)
                turn_x2(b)
                pe.wait_ge(sm["x1_done"], b.n + 1)
                route(b)

            steps(pe, first, step, last)

            pe.wait_ge(sm["onehot_done"], 1)
            t.matmul(BANK_B[:, 0:NB * E], before[:], onehot[:].rearrange("p b e -> p (b e)"), start=True, stop=False)
            pe.wait_ge(sm["seen_done"], 1)
            pe.wait_ge(sm["table"], 4 + 2 * SCAN)
            t.matmul(BANK_B[:, 0:NB * E], ones[:], seen[:, SCAN % 2, 0:NB].rearrange("p b e -> p (b e)"),
                     start=False, stop=True).then_inc(sm["rank_ready"], 1)
            t.matmul(BANK_A[:, 0:E], ones[:], seen[:, SCAN % 2, NB], start=True, stop=True).then_inc(sm["total_ready"], 1)
            for b in range(NB):
                pe.wait_ge(sm["hot_done"], 2 * b + 2)
                ins = t.matmul(BANK_B[:, 0:P], code_tok[:, b], place_hot[:, b], start=(b == 0), stop=(b == NB - 1))
            ins.then_inc(sm["ids_T_ready"], 1)
            pe.wait_ge(sm["ids_T_done"], 1)
            pe.wait_ge(sm["code_done"], 1)
            t.matmul(BANK_A[:, 0:SLOTS_W], ids_T[:], code_hot[:], start=True, stop=True).then_inc(sm["ids_ready"], 1)

            pe.wait_ge(sm["w1_in"], 16 * E)
            pe.wait_ge(sm["w2_in"], 16 * E)
            pe.wait_ge(sm["ids_taken"], 1)
            pe.wait_ge(sm["slots_done"], 1)

            def turn_xe(s, p, j):
                pe.wait_ge(gathered_in[p], (j + 1) * 16)
                if not (isinstance(s, int) and s == 0):
                    pe.wait_ge(sm["xeT_taken"], s)
                for c in range(KC):
                    ins = t.transpose(BANK_A[:, P * c:P * (c + 1)], gathered[:, p, D + P * c:D + P * (c + 1)], ident[:])
                ins.then_inc(sm["xeT_ready"], 1)

            def up(s, p, e):
                pe.wait_ge(sm["xeT_taken"], s + 1)
                for n in range(2):
                    for c in range(KC):
                        ins = t.matmul(S_BANK[n][:], xeT[:, p, c],
                                       w1_flat[:, bass.ds(e * (KC * F) + (c * F + 512 * n), 512)],
                                       start=(c == 0), stop=(c == KC - 1))
                    ins.then_inc(sm["h_ready"], 1)

            def turn_h(s):
                for c in range(FC):
                    if c % 4 == 0:
                        pe.wait_ge(sm["h_taken"], s * 2 + (c // 4 + 1))
                    ins = t.transpose(T_BANK[c // 4][:, P * (c % 4):P * (c % 4 + 1)], h_sb[:, P * c:P * (c + 1)],
                                      ident[:])
                    if c % 4 == 3:
                        ins.then_inc(sm["hT_ready"], 1)

            def down(s, p, e):
                for c in range(FC):
                    if c % 4 == 0:
                        pe.wait_ge(sm["gelu_done"], s * 2 + (c // 4 + 1))
                    ins = t.matmul(Y_BANK[p][:, 0:D], hT[:, c],
                                   w2_flat[:, bass.ds(e * (FC * D) + c * D, D)],
                                   start=(c == 0), stop=(c == FC - 1))
                ins.then_inc(sm["ye_ready"], 1)

            w1_flat = w1_sb[:].rearrange("p e c f -> p (e c f)")
            w2_flat = w2_sb[:].rearrange("p e c d -> p (e c d)")
            with nc.tensor.register("slot_expert_0") as reg0, nc.tensor.register("slot_expert_1") as reg1:
                def expert_of(reg, s):
                    t.reg_load(reg, slot_e_i[0:1, bass.ds(s, 1)])
                    return nc.s_assert_within(t.snap(reg), 0, E - 1)

                turn_xe(0, 0, 0)
                turn_xe(1, 1, 0)
                up(0, 0, expert_of(reg0, 0))
                turn_h(0)
                assert SLOTS % 2 == 1
                with pe.Fori(0, SLOTS // 2 - 1) as j:
                    s = j * 2
                    up(s + 1, 1, expert_of(reg1, s + 1))
                    down(s, 0, expert_of(reg0, s))
                    turn_xe(s + 2, 0, j + 1)
                    turn_h(s + 1)
                    up(s + 2, 0, expert_of(reg0, s + 2))
                    down(s + 1, 1, expert_of(reg1, s + 1))
                    turn_xe(s + 3, 1, j + 1)
                    turn_h(s + 2)
                s = SLOTS - 3
                up(s + 1, 1, expert_of(reg1, s + 1))
                down(s, 0, expert_of(reg0, s))
                turn_xe(s + 2, 0, s // 2 + 1)
                turn_h(s + 1)
                up(s + 2, 0, expert_of(reg0, s + 2))
                down(s + 1, 1, expert_of(reg1, s + 1))
                turn_h(s + 2)
                down(s + 2, 0, expert_of(reg0, s + 2))


def kernel(x, ctx_1024, L0_xattn_Wq, L0_xattn_bq, L0_xattn_Wk, L0_xattn_bk, L0_xattn_Wv, L0_xattn_bv, L0_xattn_Wo,
           L0_xattn_bo, L0_ffn_wr, L0_ffn_br, L0_ffn_w1, L0_ffn_b1, L0_ffn_w2, L0_ffn_b2):
    import numpy as np
    import concourse.bacc as bacc
    from concourse.bass_utils import run_bass_kernel_spmd as run

    x = np.asarray(x)
    E, F = np.asarray(L0_ffn_b1).shape
    arrays = {
        "x": x,
        "ctxT": np.asarray(ctx_1024).transpose(0, 2, 1),
        "wqT": np.asarray(L0_xattn_Wq).T, "bqT": np.asarray(L0_xattn_bq).reshape(-1, 128).T,
        "wkT": np.asarray(L0_xattn_Wk).T, "bkT": np.asarray(L0_xattn_bk).reshape(-1, 128).T,
        "wvT": np.asarray(L0_xattn_Wv).T, "bv": L0_xattn_bv,
        "woT": np.asarray(L0_xattn_Wo).T, "bo": L0_xattn_bo,
        "wr": L0_ffn_wr, "br": L0_ffn_br,
        "w1": L0_ffn_w1, "b1T": np.asarray(L0_ffn_b1).reshape(E * F // 128, 128).T,
        "w2": L0_ffn_w2, "b2": np.asarray(L0_ffn_b2).reshape(-1),
    }
    arrays = {k: np.ascontiguousarray(v) for k, v in arrays.items()}
    nc = bacc.Bacc("TRN2", target_bir_lowering=False, num_devices=1)
    args = [nc.dram_tensor(f"in_{k}", v.shape, F32, kind="ExternalInput").ap() for k, v in arrays.items()]
    out = nc.dram_tensor("out", [x.shape[0] * x.shape[1], x.shape[2]], F32, kind="ExternalOutput").ap()
    cross_attention_moe_kernel(nc, *args, out)
    r = run(nc, [{f"in_{k}": v for k, v in arrays.items()}], core_ids=[0])
    return r.results[0]["out"].reshape(x.shape)
```

```python
from contextlib import ExitStack

import concourse.bass as bass
from concourse import mybir

ALU = mybir.AluOpType
ACT = mybir.ActivationFunctionType
AX_X = mybir.AxisListType.X
F32 = mybir.dt.float32
F16 = mybir.dt.float16
BF16 = mybir.dt.bfloat16
I32 = mybir.dt.int32


class Batch:

    def __init__(self, half, parity):
        self.half, self.p, self.n = half, parity, half * 2 + parity


def cross_attention_moe_kernel(nc, x, ctxT, wqT, bqT, wkT, bkT, wvT, bv, woT, bo, wr, br, w1, b1T, w2, b2, out):
    NB, S, D = x.shape
    P = 128
    KC = D // P
    HEADS = 16
    HD = D // HEADS
    HG = P // HD
    QUAD = 4
    NQ = HEADS // QUAD
    E, _, F = w1.shape
    FC = F // P
    NTOK = NB * S
    TILES = NTOK // P
    SLOTS = (NTOK + E * (P - 1)) // P
    SLOTS_W = SLOTS + SLOTS % 2
    EPS = 1e-5
    SCALE = float(HD) ** -0.5
    NEWTON_STEPS = 3
    NEWTON_OPS = 3 + 3 * NEWTON_STEPS
    RSQRT_MAGIC = 0x5F3759DF
    OUT_OF_BOUNDS = 2 * NTOK
    PARTS = 3
    PRODUCTS = PARTS * (PARTS + 1) // 2
    SR = PRODUCTS * HD
    assert S == P and D == KC * P and E * TILES == P

    with ExitStack() as ctx:
        def sb(name, shape, dt=F32):
            return ctx.enter_context(nc.sbuf_tensor(name, shape, dt))

        def psum(name, shape, dt=F32):
            return ctx.enter_context(nc.psum_tensor(name, shape, dt))

        def sem(name):
            return ctx.enter_context(nc.semaphore(name))

        w1_sb = sb("w1_sb", [P, E, KC, F])
        w2_sb = sb("w2_sb", [P, E, FC, D])
        b1_sb = sb("b1_sb", [P, E * FC])
        wq_sb = sb("wq_sb", [P, KC, D])
        wk_sb = sb("wk_sb", [P, KC, D])
        wv_sb = sb("wv_sb", [P, KC, D])
        wo_sb = sb("wo_sb", [P, KC, D])
        wr_sb = sb("wr_sb", [P, KC, E])
        bq_sb = sb("bq_sb", [P, KC])
        bk_sb = sb("bk_sb", [P, KC])
        bv_sb = sb("bv_sb", [P, D])
        bo_sb = sb("bo_sb", [P, D])
        br_sb = sb("br_sb", [P, E])
        ident = sb("ident", [P, P])
        earlier = sb("earlier", [P, P], F16)
        ones = sb("ones", [P, P], F16)
        iota_i = sb("iota_i", [P, P], I32)
        iota_row = sb("iota_row", [P, P])
        iota_part_i = sb("iota_part_i", [P, 1], I32)
        iota_part = sb("iota_part", [P, 1])
        rev_i = sb("rev_i", [P, E], I32)
        rev = sb("rev", [P, E])
        zero = sb("zero", [P, 1])
        tok_i = sb("tok_i", [P, NB], I32)
        tok1 = sb("tok1", [P, NB])

        x_sb = sb("x_sb", [P, 2, D])
        xb_sb = sb("xb_sb", [P, 2, D])
        ctx_sb = sb("ctx_sb", [P, 2, KC, P])
        xn = sb("xn", [P, D])
        xnT = sb("xnT", [P, KC, P])
        qT = sb("qT", [P, KC, P])
        kT = sb("kT", [P, KC, P])
        q_parts = sb("q_parts", [P, PARTS, KC * P], BF16)
        k_parts = sb("k_parts", [P, PARTS, KC * P], BF16)
        stacks = sb("stacks", [P, 2, HG, KC, P], BF16)
        q_stack, k_stack = stacks[:, 0], stacks[:, 1]
        v_diag = sb("v_diag", [P, 2, KC, HG, P])
        probs = sb("probs", [P, HEADS, P])
        probsT = sb("probsT", [P, 2, QUAD * P])
        row_max = sb("row_max", [P, HEADS])
        neg_max = sb("neg_max", [P, HEADS])
        sums = sb("sums", [P, 2, HEADS])
        recips = sb("recips", [P, HEADS])
        recips_d = sb("recips_d", [P, HEADS, HD])
        recipsT = sb("recipsT", [P, KC, P])
        oT = sb("oT", [P, 2, KC, P])
        record = sb("record", [P, 2, 2 * D])
        x2T = sb("x2T", [P, KC, P])
        stats = sb("stats", [P, 2, 6])
        mean_var = sb("mean_var", [P, 2, 2])
        nw_y = sb("nw_y", [P, 2])
        nw_i = sb("nw_i", [P, 2], I32)
        nw_v = sb("nw_v", [P, 2])
        nw_t = sb("nw_t", [P, 2])
        nw_u = sb("nw_u", [P, 2])
        logits = sb("logits", [P, NB, E])
        best = sb("best", [P, NB])
        keyed = sb("keyed", [P, NB, E])
        key = sb("key", [P, NB])
        onehot = sb("onehot", [P, NB, E], F16)
        ranked = sb("ranked", [P, NB, E])
        rank, place, e_code, code = (sb(n, [P, NB]) for n in ("rank", "place", "e_code", "code"))
        rank_i, tile_i, place_i = (sb(n, [P, NB], I32) for n in ("rank_i", "tile_i", "place_i"))
        hots = probs[:].bitcast(F16).rearrange("p (o h) k -> p o (h k)", o=2)
        place_hot, code_tok = (hots[:, i].rearrange("p (b k) -> p b k", k=P) for i in range(2))

        PAD = E
        n_i = sb("n_i", [P, E], I32)
        n_sh = sb("n_sh", [P, E], I32)
        n_f = sb("n_f", [P, E])
        ends = sb("ends", [P, 4, PAD + E])
        slot_i = sb("slot_i", [P, SLOTS_W], I32)
        slot_f = sb("slot_f", [P, SLOTS_W])
        passed, passed_n = (probsT[:, i, 0:SLOTS_W * E].rearrange("p (s e) -> p s e", e=E) for i in range(2))
        slot_e = sb("slot_e", [P, SLOTS_W])
        slot_start = sb("slot_start", [P, SLOTS_W])
        slot_e_i = sb("slot_e_i", [P, SLOTS_W], I32)
        slot_c = sb("slot_c", [P, SLOTS_W])
        slot_code = sb("slot_code", [P, SLOTS_W])
        code_hot = sb("code_hot", [P, SLOTS_W], F16)
        ids_T = sb("ids_T", [P, P], F16)
        ids = sb("ids", [P, SLOTS_W])
        ids_pad = sb("ids_pad", [P, SLOTS_W])
        gather_i = sb("gather_i", [P, SLOTS_W], I32)
        scatter_i = sb("scatter_i", [P, SLOTS_W], I32)
        g_idx = sb("g_idx", [P, 2, 1], I32)
        s_idx = sb("s_idx", [P, 2, 1], I32)

        spare = v_diag[:].rearrange("p b c h s -> p (b c h s)")
        gathered = spare[:, 0:4 * D].rearrange("p (b d) -> p b d", b=2)
        xeT = spare[:, 4 * D:6 * D].rearrange("p (b c s) -> p b c s", b=2, c=KC)
        hT = spare[:, 6 * D:6 * D + F].rearrange("p (c s) -> p c s", c=FC)
        h_sb = probsT[:].rearrange("p b k -> p (b k)")
        y_sb = record[:, 0].rearrange("p (b d) -> p b d", b=2)
        x1_b2 = record[:, 1].rearrange("p (b d) -> p b d", b=2)
        b2_sb = stacks[:].rearrange("p o h c s -> p (o h c s)").bitcast(F32)[:, 0:E * D]

        banks = [psum(f"bank{i}", [P, 512]) for i in range(8)]
        S_BANK, O_BANK, T_BANK = banks[0:3], banks[3], banks[4:6]
        Y_BANK = banks[2:4]
        BANK_A, BANK_B = banks[6], banks[7]

        records = nc.dram_tensor("records", [NTOK, 2 * D], F32).ap()
        q_turn, k_turn = (nc.dram_tensor(n, [PARTS * HD, HG * KC * P], BF16).ap() for n in ("q_turn", "k_turn"))

        names = """consts_pool consts_dve wq_in wk_in wv_in wo_in wr_in bias_in w1_in w2_in b2_in
            xb_done xT_ready xT_taken k_ready q_ready v_ready k_taken q_taken v_taken k_parted q_parted
            k_turned q_turned k_stacked q_stacked
            stats1 aggr1 stats2 aggr2 newton xn_done xn2_done scores_ready max_done neg_done exp_done
            probsT_ready probsT_taken values_weighed recip_done recip_d_done rT_ready rT_taken oT_done
            y_ready x1_done x2T_ready x2T_taken logits_ready logits_taken
            onehot_done rank_ready total_ready table codes_done place_hot_done code_tok_pool code_tok_dve code_hot_done
            ids_T_ready ids_T_done ids_ready ids_taken index_done slots_done
            gather_idx_copied scatter_idx_copied xeT_ready xeT_taken h_ready h_taken hT_ready gelu_done ye_ready ye_done
            b2_done""".split()
        sm = {n: sem(n) for n in names}
        x_in = [sem("x_in0"), sem("x_in1")]
        xb_in = [sem("xb_in0"), sem("xb_in1")]
        ctx_in = [sem("ctx_in0"), sem("ctx_in1")]
        record_out = [sem("record_out0"), sem("record_out1")]
        gathered_in = [sem("gathered_in0"), sem("gathered_in1")]
        y_out = [sem("y_out0"), sem("y_out1")]

        STACKED = 16 * PARTS
        DVE_ROWS = 5 * NB // 8
        EARLY = range(NQ - 1)

        def held(eng, value):
            return value if isinstance(value, int) else eng.to_reg(value)

        def steps(eng, first, step, last):
            def run(b, nxt, after, prev, before):
                seq = [Batch(*v) if v is not None else None for v in (b, nxt, after, prev, before)]
                step(*seq)

            first()
            run((0, 0), (0, 1), (1, 0), None, None)
            run((0, 1), (1, 0), (1, 1), (0, 0), None)
            run((1, 0), (1, 1), (2, 0), (0, 1), (0, 0))
            with eng.Fori(1, NB // 2 - 2) as j:
                run((j, 1), (j + 1, 0), (j + 1, 1), (j, 0), (j - 1, 1))
                run((j + 1, 0), (j + 1, 1), (j + 2, 0), (j, 1), (j, 0))
            h = NB // 2 - 1
            run((h - 1, 1), (h, 0), (h, 1), (h - 1, 0), (h - 2, 1))
            run((h, 0), (h, 1), None, (h - 1, 1), (h - 1, 0))
            run((h, 1), None, None, (h, 0), (h - 1, 1))
            last(Batch(h, 0), Batch(h, 1))

        def slots(eng, body):
            assert SLOTS % 2 == 1
            body(0, 0, 0)
            with eng.Fori(0, SLOTS // 2) as j:
                body(j * 2 + 1, 1, j)
                body(j * 2 + 2, 0, j + 1)

        block = ctx.enter_context(nc.Block())

        @block.sync
        def _(sp):
            def load(b):
                sp.dma_start(ctx_sb[:, b.p], ctxT[bass.ds(b.n, 1)].rearrange("o (c p) s -> p (o c) s", p=P))\
                    .then_inc(ctx_in[b.p], 16)
                sp.dma_start(x_sb[:, b.p], x[bass.ds(b.n, 1)].rearrange("o p d -> p (o d)")).then_inc(x_in[b.p], 16)

            def load_third(old):
                sp.wait_ge(sm["v_ready"], old.n + 1)
                sp.wait_ge(sm["xn_done"], old.n + 1)
                load(Batch(old.half + 1, old.p))

            def load_residual(b):
                if not (isinstance(b.n, int) and b.n < 2):
                    sp.wait_ge(sm["x1_done"], b.n - 1)
                sp.dma_start(xb_sb[:, b.p], x[bass.ds(b.n, 1)].rearrange("o p d -> p (o d)")).then_inc(xb_in[b.p], 16)

            def turn_parts(b, parts, turned, taken, parted, turn, stacked):
                out = turned.rearrange("(t d) (h f) -> t h d f", t=PARTS, h=HG)
                for i in range(PARTS):
                    if i == 0:
                        first_part, before_it = held(sp, b.n + 1), held(sp, b.n * STACKED)
                        sp.wait_ge(sm[taken], first_part)
                        if not (isinstance(b.n, int) and b.n == 0):
                            sp.wait_ge(sm[stacked], before_it)
                    else:
                        sp.wait_ge(sm[parted], b.n * PARTS + (i + 1))
                    sp.dma_start(out[i], parts[:, i]).then_inc(sm[turn], 16)

            def stack(b, dst, turned, turn, stacked, is_q):
                done, scored = held(sp, (b.n + 1) * STACKED), held(sp, b.n * NQ)
                sp.wait_ge(sm[turn], done)
                if not (isinstance(b.n, int) and b.n == 0):
                    sp.wait_ge(sm["scores_ready"], scored)
                row = 0
                for i in range(PARTS):
                    n = (PARTS - i) * HD
                    if is_q:
                        src = turned.rearrange("(t d) f -> t d f", t=PARTS)[i:i + 1]\
                            .broadcast_to([PARTS - i, HD, HG * KC * P])
                    else:
                        src = turned[0:n]
                    sp.dma_start(dst[row:row + n].rearrange("p h c s -> p (h c s)"), src).then_inc(sm[stacked], 16)
                    row += n

            def turn(b):
                turn_parts(b, k_parts, k_turn, "k_taken", "k_parted", "k_turned", "k_stacked")
                turn_parts(b, q_parts, q_turn, "q_taken", "q_parted", "q_turned", "q_stacked")

            def stacks_of(b):
                stack(b, k_stack, k_turn, "k_turned", "k_stacked", False)
                stack(b, q_stack, q_turn, "q_turned", "q_stacked", True)

            def save_record(b):
                sp.wait_ge(sm["xn2_done"], b.n + 1)
                sp.dma_start(records[bass.ds(b.n * P, P), :], record[:, b.p]).then_inc(record_out[b.p], 16)

            def first():
                for b, names in ((Batch(0, 0), (("wk_in", wk_sb, wkT), ("wv_in", wv_sb, wvT), ("wq_in", wq_sb, wqT))),
                                 (Batch(0, 1), (("wo_in", wo_sb, woT),))):
                    load(b)
                    for name, dst, src in names:
                        sp.dma_start(dst[:], src.rearrange("(c p) n -> p c n", p=P)).then_inc(sm[name], 16)
                sp.dma_start(wr_sb[:], wr.rearrange("(c p) e -> p c e", p=P)).then_inc(sm["wr_in"], 16)
                turn(Batch(0, 0))
                stacks_of(Batch(0, 0))
                load_third(Batch(0, 0))
                turn(Batch(0, 1))

            def step(b, nxt, after, prev, before):
                if nxt is not None:
                    stacks_of(nxt)
                load_residual(b)
                if before is not None:
                    save_record(before)
                if not isinstance(b.n, int) or b.n + 3 < NB:
                    load_third(nxt)
                if after is not None:
                    turn(after)

            def last(prev, b):
                save_record(prev)
                save_record(b)
                sp.dma_start(b2_sb, b2.rearrange("(o n) -> o n", o=1).broadcast_to([P, E * D]))\
                    .then_inc(sm["b2_in"], 16)

            steps(sp, first, step, last)

        @block.gpsimd
        def _(pool):
            g = nc.gpsimd
            g.memset(v_diag[:], 0.0)
            g.memset(ident[:], 0.0)
            g.memset(earlier[:], 1.0)
            g.memset(ends[:], 0.0).then_inc(sm["consts_pool"], 1)
            pool.wait_ge(sm["consts_pool"], 1)
            g.affine_select(out=ident[:], in_=ident[:], compare_op=ALU.not_equal, fill=1.0, base=0,
                            pattern=[[-1, P]], channel_multiplier=1)
            g.affine_select(out=earlier[:], in_=earlier[:], compare_op=ALU.is_ge, fill=0.0, base=-1,
                            pattern=[[1, P]], channel_multiplier=-1)
            g.memset(ones[:], 1.0)
            g.memset(zero[:], 0.0)
            g.iota(iota_i[:], pattern=[[1, P]], base=0, channel_multiplier=0)
            g.iota(iota_part_i[:], pattern=[[1, 1]], base=0, channel_multiplier=1)
            g.iota(rev_i[:], pattern=[[-1, E]], base=E, channel_multiplier=0)
            g.iota(tok_i[:], pattern=[[P, NB]], base=1, channel_multiplier=1)
            g.iota(slot_i[:], pattern=[[1, SLOTS_W]], base=0, channel_multiplier=0).then_inc(sm["consts_pool"], 1)
            pool.wait_ge(sm["consts_pool"], 2)
            g.tensor_copy(iota_row[:], iota_i[:])
            g.tensor_copy(iota_part[:], iota_part_i[:])
            g.tensor_copy(rev[:], rev_i[:])
            g.tensor_copy(tok1[:], tok_i[:])
            g.tensor_copy(slot_f[:], slot_i[:]).then_inc(sm["consts_pool"], 1)

            def add_bo(b):
                pool.wait_ge(xb_in[b.p], (b.half + 1) * 16)
                g.tensor_tensor(xb_sb[:, b.p], xb_sb[:, b.p], bo_sb[:], ALU.add).then_inc(sm["xb_done"], 1)

            def split(b, whole, parts, taken, parted):
                flat = whole[:].rearrange("p c s -> p (c s)")
                pool.wait_ge(sm[taken], b.n + 1)
                g.tensor_tensor(flat, flat, parts[:, 0], ALU.subtract).then_inc(sm[parted], 1)
                pool.wait_ge(sm[parted], b.n * PARTS + 1)
                g.tensor_tensor(parts[:, 1], flat, zero[:].broadcast_to([P, KC * P]), ALU.add)\
                    .then_inc(sm[parted], 1)
                pool.wait_ge(sm[parted], b.n * PARTS + 2)
                g.tensor_tensor(parts[:, 2], flat, parts[:, 1], ALU.subtract).then_inc(sm[parted], 1)

            def first():
                pool.wait_ge(sm["bias_in"], 16 * 6)
                for b in (Batch(0, 0), Batch(0, 1)):
                    split(b, kT, k_parts, "k_taken", "k_parted")
                    split(b, qT, q_parts, "q_taken", "q_parted")

            def step(b, nxt, after, prev, before):
                if after is not None:
                    split(after, kT, k_parts, "k_taken", "k_parted")
                    split(after, qT, q_parts, "q_taken", "q_parted")
                add_bo(b)

            steps(pool, first, step, lambda prev, b: None)

            def scatter(s, p, j):
                if not (isinstance(j, int) and j == 0):
                    pool.wait_ge(y_out[p], j * 16)
                g.tensor_copy(s_idx[:, p], scatter_i[:, bass.ds(s, 1)]).then_inc(sm["scatter_idx_copied"], 1)
                count = held(pool, s + 1)
                pool.wait_ge(sm["index_done"], 2)
                pool.wait_ge(sm["scatter_idx_copied"], count)
                pool.wait_ge(sm["ye_done"], count)
                g.indirect_dma_start(out=out[:, :], out_offset=bass.IndirectOffsetOnAxis(ap=s_idx[:, p], axis=0),
                                     in_=y_sb[:, p], in_offset=None, bounds_check=NTOK - 1, oob_is_err=False)\
                    .then_inc(y_out[p], 16)

            def gather(s, p, wait_used=True):
                if wait_used:
                    pool.wait_ge(sm["b2_done"], s - 1)
                    pool.wait_ge(sm["xeT_taken"], s - 1)
                g.tensor_copy(g_idx[:, p], gather_i[:, bass.ds(s, 1)]).then_inc(sm["gather_idx_copied"], 1)
                copied = held(pool, s + 1)
                pool.wait_ge(sm["index_done"], 1)
                pool.wait_ge(sm["gather_idx_copied"], copied)
                g.indirect_dma_start(out=gathered[:, p], out_offset=None, in_=records[:, :],
                                     in_offset=bass.IndirectOffsetOnAxis(ap=g_idx[:, p], axis=0))\
                    .then_inc(gathered_in[p], 16)

            pool.wait_ge(sm["codes_done"], 1)
            for b in range(DVE_ROWS, NB):
                g.tensor_scalar(code_tok[:, b], iota_row[:], code[:, b:b + 1], tok1[:, b:b + 1], ALU.is_equal,
                                ALU.mult).then_inc(sm["code_tok_pool"], 1)

            pool.wait_ge(sm["index_done"], 1)
            for p in range(2):
                pool.wait_ge(record_out[p], 16 * (NB // 2))
            gather(0, 0, False)
            gather(1, 1, False)
            gather(2, 0)
            scatter(0, 0, 0)
            gather(3, 1)
            scatter(1, 1, 0)
            with pool.Fori(1, (SLOTS - 2) // 2) as j:
                gather(j * 2 + 2, 0)
                scatter(j * 2, 0, j)
                gather(j * 2 + 3, 1)
                scatter(j * 2 + 1, 1, j)
            done = (SLOTS - 2) // 2 * 2
            for s in range(done, SLOTS):
                if s + 2 < SLOTS:
                    gather(s + 2, s % 2)
                scatter(s, s % 2, s // 2)
            pool.wait_ge(y_out[0], 16 * ((SLOTS + 1) // 2))
            pool.wait_ge(y_out[1], 16 * (SLOTS // 2))

        @block.scalar
        def _(act):
            a = nc.scalar

            def rep(v, n):
                return v.rearrange("(o n) -> o n", o=1).broadcast_to([P, n])

            act.dma_start(bk_sb[:], bkT).then_inc(sm["bias_in"], 16)
            act.dma_start(bq_sb[:], bqT).then_inc(sm["bias_in"], 16)
            act.dma_start(bv_sb[:], rep(bv, D)).then_inc(sm["bias_in"], 16)
            act.dma_start(bo_sb[:], rep(bo, D)).then_inc(sm["bias_in"], 16)
            act.dma_start(br_sb[:], rep(br, E)).then_inc(sm["bias_in"], 16)
            act.dma_start(b1_sb[:], b1T).then_inc(sm["bias_in"], 16)

            def load_expert(b):
                e = bass.ds(b.half, 1)
                if b.p == 0:
                    act.dma_start(w1_sb[:, e].rearrange("p o c f -> p (o c) f"),
                                  w1[e].rearrange("o (c p) f -> p (o c) f", p=P)).then_inc(sm["w1_in"], 16)
                else:
                    act.dma_start(w2_sb[:, e].rearrange("p o c d -> p (o c) d"),
                                  w2[e].rearrange("o (c p) d -> p (o c) d", p=P)).then_inc(sm["w2_in"], 16)

            def exps(b, q):
                act.wait_ge(sm["neg_done"], b.n * NQ + (q + 1))
                for i in range(QUAD):
                    h = QUAD * q + i
                    ins = a.activation(probs[:, h], S_BANK[q % 3][:, P * i:P * (i + 1)], ACT.Exp, scale=SCALE,
                                       bias=neg_max[:, h:h + 1], accum_out=sums[:, b.p, h:h + 1])
                ins.then_inc(sm["exp_done"], 1)

            def take_split(b, ready, turned, taken, bank, bias, whole, parts):
                act.wait_ge(sm[ready], b.n + 1)
                if not (isinstance(b.n, int) and b.n == 0):
                    act.wait_ge(sm[turned], b.n * STACKED)
                for c in range(KC):
                    a.activation(parts[:, 0, P * c:P * (c + 1)], bank[:, P * c:P * (c + 1)], ACT.Identity,
                                 bias=bias[:, c:c + 1])
                for c in range(KC):
                    ins = a.activation(whole[:, c], bank[:, P * c:P * (c + 1)], ACT.Identity, bias=bias[:, c:c + 1])
                ins.then_inc(sm[taken], 1)

            def take_k(b):
                take_split(b, "k_ready", "k_turned", "k_taken", BANK_B, bk_sb, kT, k_parts)

            def take_q(b):
                take_split(b, "q_ready", "q_turned", "q_taken", BANK_A, bq_sb, qT, q_parts)

            def take_xT(b):
                act.wait_ge(sm["xT_ready"], b.n + 1)
                a.copy(xnT[:], BANK_A[:, 0:D].rearrange("p (c s) -> p c s", c=KC)).then_inc(sm["xT_taken"], 1)

            def take_x2T(b):
                act.wait_ge(sm["x2T_ready"], b.n + 1)
                a.copy(x2T[:], BANK_B[:, 0:D].rearrange("p (c s) -> p c s", c=KC)).then_inc(sm["x2T_taken"], 1)

            def take_probsT(b, q):
                act.wait_ge(sm["probsT_ready"], b.n * NQ + (q + 1))
                if q >= 2 or not (isinstance(b.n, int) and b.n == 0):
                    act.wait_ge(sm["values_weighed"], b.n * NQ + (q - 1))
                a.copy(probsT[:, q % 2], T_BANK[q % 2][:]).then_inc(sm["probsT_taken"], 1)

            def take_rT(b):
                act.wait_ge(sm["rT_ready"], b.n + 1)
                a.copy(recipsT[:], O_BANK[:, D:2 * D].rearrange("p (c s) -> p c s", c=KC)).then_inc(sm["rT_taken"], 1)

            def first():
                act.wait_ge(sm["bias_in"], 16 * 6)
                for b in (Batch(0, 0), Batch(0, 1)):
                    take_k(b)
                    take_xT(b)
                    take_q(b)
                for q in EARLY:
                    exps(Batch(0, 0), q)

            def step(b, nxt, after, prev, before):
                take_probsT(b, 0)
                exps(b, NQ - 1)
                take_probsT(b, 1)
                take_probsT(b, 2)
                if after is not None:
                    take_xT(after)
                take_probsT(b, 3)
                if after is not None:
                    take_k(after)
                load_expert(b)
                if nxt is not None:
                    exps(nxt, 0)
                if after is not None:
                    take_q(after)
                if before is not None:
                    take_x2T(before)
                take_rT(b)
                if nxt is not None:
                    exps(nxt, 1)
                    exps(nxt, 2)

            def last(prev, b):
                take_x2T(prev)
                take_x2T(b)

            steps(act, first, step, last)

            with nc.scalar.register("slot_expert_act") as reg:
                def expert_gelu(s, p, j):
                    a.reg_load(reg, slot_e_i[0:1, bass.ds(s, 1)])
                    e = nc.s_assert_within(a.snap(reg), 0, E - 1)
                    for c in range(FC):
                        if c % 4 == 0:
                            act.wait_ge(sm["hT_ready"], s * 2 + (c // 4 + 1))
                        ins = a.activation(hT[:, c], T_BANK[c // 4][:, P * (c % 4):P * (c % 4 + 1)], ACT.Gelu,
                                           bias=b1_sb[:, bass.ds(e * FC + c, 1)])
                        if c % 4 == 3:
                            ins.then_inc(sm["gelu_done"], 1)
                act.wait_ge(sm["slots_done"], 1)
                slots(act, expert_gelu)

        @block.vector
        def _(dve):
            v = nc.vector
            LN2, LN1 = 0, 1

            def stats_of(src, col, name, count):
                count = held(dve, count)
                v.bn_stats(stats[:, col], src).then_inc(sm["stats" + name], 1)
                dve.wait_ge(sm["consts_dve"], 1)
                dve.wait_ge(sm["stats" + name], count)
                v.bn_aggr(mean_var[:, col], stats[:, col]).then_inc(sm["aggr" + name], 1)

            def stats_x(b):
                dve.wait_ge(x_in[b.p], (b.half + 1) * 16)
                if not isinstance(b.n, int) or b.n > 0:
                    dve.wait_ge(sm["xn_done"], b.n)
                stats_of(x_sb[:, b.p], LN1, "1", b.n + 1)

            def inverse_roots(turn):
                n = [0]

                def link(ins):
                    n[0] += 1
                    ins.then_inc(sm["newton"], 1)
                    dve.wait_ge(sm["newton"], turn * NEWTON_OPS + n[0])

                link(v.tensor_scalar(nw_v[:], mean_var[:, :, 1], EPS, None, ALU.add))
                link(v.tensor_scalar(nw_i[:], nw_v[:].bitcast(I32), 1, None, ALU.logical_shift_right))
                link(v.tensor_scalar(nw_y[:].bitcast(I32), nw_i[:], -1, RSQRT_MAGIC, ALU.mult, ALU.add))
                for _ in range(NEWTON_STEPS):
                    link(v.tensor_tensor(nw_t[:], nw_y[:], nw_y[:], ALU.mult))
                    link(v.scalar_tensor_tensor(out=nw_u[:], in0=nw_t[:], scalar=-0.5, in1=nw_v[:],
                                                op0=ALU.mult, op1=ALU.mult))
                    link(v.scalar_tensor_tensor(out=nw_y[:], in0=nw_u[:], scalar=1.5, in1=nw_y[:],
                                                op0=ALU.add, op1=ALU.mult))

            def normalize(dst, src, col, done):
                v.tensor_scalar(dst, src, mean_var[:, col, 0:1], nw_y[:, col:col + 1],
                                ALU.subtract, ALU.mult).then_inc(done, 1)

            def maxima(b, q):
                dve.wait_ge(sm["scores_ready"], b.n * NQ + (q + 1))
                hs = slice(QUAD * q, QUAD * (q + 1))
                v.tensor_reduce(row_max[:, hs], S_BANK[q % 3][:].rearrange("p (h k) -> p h k", k=P), AX_X,
                                ALU.max).then_inc(sm["max_done"], 1)
                dve.wait_ge(sm["max_done"], b.n * NQ + (q + 1))
                v.tensor_scalar(neg_max[:, hs], row_max[:, hs], -SCALE, None, ALU.mult).then_inc(sm["neg_done"], 1)

            def residual(b):
                dve.wait_ge(sm["y_ready"], b.n + 1)
                dve.wait_ge(sm["xb_done"], b.n + 1)
                if not isinstance(b.n, int) or b.n >= 2:
                    dve.wait_ge(record_out[b.p], b.half * 16)
                v.tensor_tensor(record[:, b.p, 0:D], BANK_A[:, 0:D], xb_sb[:, b.p], ALU.add)\
                    .then_inc(sm["x1_done"], 1)

            def stats_x1(b):
                dve.wait_ge(sm["x1_done"], b.n + 1)
                stats_of(record[:, b.p, 0:D], LN2, "2", b.n + 1)

            def take_v(b):
                dve.wait_ge(sm["v_ready"], b.n + 1)
                for c in range(KC):
                    blocks = v_diag[:, b.p, c].rearrange("p h (i d) -> p (h i) d", d=HD)[:, ::HG + 1, :]
                    ins = v.tensor_tensor(blocks, BANK_B[:, P * c:P * (c + 1)].rearrange("p (h d) -> p h d", d=HD),
                                          bv_sb[:, P * c:P * (c + 1)].rearrange("p (h d) -> p h d", d=HD), ALU.add)
                ins.then_inc(sm["v_taken"], 1)

            def take_logits(b):
                dve.wait_ge(sm["logits_ready"], b.n + 1)
                v.tensor_tensor(logits[:, bass.ds(b.n, 1)].rearrange("p o e -> p (o e)"), BANK_A[:, 0:E], br_sb[:],
                                ALU.add).then_inc(sm["logits_taken"], 1)

            def reciprocals(b):
                dve.wait_ge(sm["exp_done"], (b.n + 1) * NQ)
                v.reciprocal(recips[:], sums[:, b.p]).then_inc(sm["recip_done"], 1)
                dve.wait_ge(sm["recip_done"], b.n + 1)
                v.tensor_copy(recips_d[:], recips[:].unsqueeze(2).broadcast_to([P, HEADS, HD]))\
                    .then_inc(sm["recip_d_done"], 1)

            def normalize_heads(b):
                dve.wait_ge(sm["rT_taken"], b.n + 1)
                dve.wait_ge(sm["values_weighed"], (b.n + 1) * NQ)
                v.tensor_tensor(oT[:, b.p], O_BANK[:, 0:D].rearrange("p (c s) -> p c s", c=KC), recipsT[:],
                                ALU.mult).then_inc(sm["oT_done"], 1)

            def first():
                v.memset(mean_var[:], 1.0).then_inc(sm["consts_dve"], 1)
                dve.wait_ge(sm["consts_dve"], 1)
                b = Batch(0, 0)
                stats_x(b)
                dve.wait_ge(sm["aggr1"], 1)
                inverse_roots(0)
                normalize(xn[:], x_sb[:, 0], LN1, sm["xn_done"])
                dve.wait_ge(sm["consts_pool"], 3)
                dve.wait_ge(sm["bias_in"], 16 * 6)
                take_v(b)
                stats_x(Batch(0, 1))
                dve.wait_ge(sm["aggr1"], 2)
                inverse_roots(1)
                dve.wait_ge(sm["xT_ready"], 1)
                normalize(xn[:], x_sb[:, 1], LN1, sm["xn_done"])
                for q in range(NQ):
                    maxima(b, q)
                stats_x(Batch(1, 0))

            def step(b, nxt, after, prev, before):
                if after is not None:
                    dve.wait_ge(sm["aggr1"], after.n + 1)
                if before is not None:
                    dve.wait_ge(sm["aggr2"], before.n + 1)
                inverse_roots(b.n + 2)
                if after is not None:
                    dve.wait_ge(sm["xT_ready"], b.n + 2)
                    normalize(xn[:], x_sb[:, after.p], LN1, sm["xn_done"])
                if prev is not None:
                    residual(prev)
                if before is not None:
                    normalize(record[:, before.p, D:2 * D], record[:, before.p, 0:D], LN2, sm["xn2_done"])
                    dve.wait_ge(sm["xn2_done"], before.n + 1)
                if nxt is not None:
                    take_v(nxt)
                if prev is not None:
                    stats_x1(prev)
                reciprocals(b)
                if nxt is not None:
                    for q in EARLY:
                        maxima(nxt, q)
                if not isinstance(b.n, int) or b.n + 3 < NB:
                    stats_x(Batch(nxt.half + 1, nxt.p))
                if before is not None:
                    take_logits(before)
                if nxt is not None:
                    maxima(nxt, NQ - 1)
                normalize_heads(b)

            def last(prev, b):
                residual(b)
                dve.wait_ge(sm["x1_done"], b.n + 1)
                stats_of(record[:, b.p, 0:D], LN1, "1", NB + 1)
                dve.wait_ge(sm["aggr1"], NB + 1)
                dve.wait_ge(sm["aggr2"], prev.n + 1)
                inverse_roots(NB + 2)
                normalize(record[:, prev.p, D:2 * D], record[:, prev.p, 0:D], LN2, sm["xn2_done"])
                normalize(record[:, b.p, D:2 * D], record[:, b.p, 0:D], LN1, sm["xn2_done"])
                take_logits(prev)
                take_logits(b)

            steps(dve, first, step, last)

            n = [0]

            def link(ins):
                n[0] += 1
                ins.then_inc(sm["table"], 1)
                dve.wait_ge(sm["table"], n[0])

            def place_row(b):
                v.tensor_scalar(place_hot[:, b], iota_row[:], place[:, b:b + 1], None, ALU.is_equal)\
                    .then_inc(sm["place_hot_done"], 1)

            def code_row(b):
                v.tensor_scalar(code_tok[:, b], iota_row[:], code[:, b:b + 1], tok1[:, b:b + 1], ALU.is_equal,
                                ALU.mult).then_inc(sm["code_tok_dve"], 1)

            def link_over(ins, b):
                n[0] += 1
                ins.then_inc(sm["table"], 1)
                place_row(b)
                if b < DVE_ROWS:
                    code_row(b)
                dve.wait_ge(sm["table"], n[0])

            by_expert = [P, NB, E]
            dve.wait_ge(sm["logits_taken"], NB)
            link(v.tensor_reduce(best[:], logits[:], AX_X, ALU.max))
            link(v.tensor_tensor(keyed[:], logits[:], best[:].unsqueeze(2).broadcast_to(by_expert), ALU.is_equal))
            link(v.tensor_tensor(keyed[:], keyed[:], rev[:].unsqueeze(1).broadcast_to(by_expert), ALU.mult))
            link(v.tensor_reduce(key[:], keyed[:], AX_X, ALU.max))
            v.tensor_tensor(onehot[:], keyed[:], key[:].unsqueeze(2).broadcast_to(by_expert), ALU.is_equal)\
                .then_inc(sm["onehot_done"], 1)
            dve.wait_ge(sm["onehot_done"], 1)
            link(v.tensor_scalar(e_code[:], key[:], -float(TILES), float(E * TILES), ALU.mult, ALU.add))
            dve.wait_ge(sm["rank_ready"], 1)
            link(v.tensor_tensor(ranked[:], BANK_B[:, 0:NB * E].rearrange("p (b e) -> p b e", e=E), onehot[:],
                                 ALU.mult))
            link(v.tensor_reduce(rank[:], ranked[:], AX_X, ALU.add))
            link(v.tensor_copy(rank_i[:], rank[:]))
            link(v.tensor_scalar(tile_i[:], rank_i[:], 7, None, ALU.logical_shift_right))
            link(v.tensor_scalar(place_i[:], rank_i[:], P - 1, None, ALU.bitwise_and))
            link(v.tensor_copy(place[:], place_i[:]))
            v.tensor_tensor(code[:], tile_i[:], e_code[:], ALU.add).then_inc(sm["codes_done"], 1)
            dve.wait_ge(sm["codes_done"], 1)
            dve.wait_ge(sm["total_ready"], 1)
            link_over(v.tensor_scalar(n_i[:], BANK_A[:, 0:E], float(P - 1), None, ALU.add), 0)
            link_over(v.tensor_scalar(n_sh[:], n_i[:], 7, None, ALU.logical_shift_right), 1)
            v.tensor_copy(n_f[:], n_sh[:])
            link_over(v.tensor_copy(ends[:, 0, PAD:], n_sh[:]), 2)
            for k, shift in enumerate((1, 2, 4)):
                link_over(v.tensor_tensor(ends[:, k + 1, PAD:], ends[:, k, PAD:],
                                          ends[:, k, PAD - shift:PAD + E - shift], ALU.add), 3 + k)
            by_slot = [P, SLOTS_W, E]
            link_over(v.tensor_tensor(passed[:], slot_f[:].unsqueeze(2).broadcast_to(by_slot),
                                      ends[:, 3, PAD:].unsqueeze(1).broadcast_to(by_slot), ALU.is_ge), 6)
            link_over(v.tensor_tensor(passed_n[:], passed[:], n_f[:].unsqueeze(1).broadcast_to(by_slot), ALU.mult), 7)
            v.tensor_reduce(slot_e[:], passed[:], AX_X, ALU.add)
            link_over(v.tensor_reduce(slot_start[:], passed_n[:], AX_X, ALU.add), 8)
            v.tensor_scalar(slot_e_i[:], slot_e[:], float(E - 1), None, ALU.min).then_inc(sm["slots_done"], 1)
            link_over(v.tensor_tensor(slot_c[:], slot_f[:], slot_start[:], ALU.subtract), 9)
            link_over(v.scalar_tensor_tensor(out=slot_code[:], in0=slot_e[:], scalar=float(TILES), in1=slot_c[:],
                                             op0=ALU.mult, op1=ALU.add), 10)
            v.tensor_scalar(code_hot[:], slot_code[:], iota_part[:], None, ALU.is_equal)\
                .then_inc(sm["code_hot_done"], 1)
            for b in range(11, NB):
                place_row(b)
            dve.wait_ge(sm["ids_T_ready"], 1)
            v.tensor_copy(ids_T[:], BANK_B[:, 0:P]).then_inc(sm["ids_T_done"], 1)
            dve.wait_ge(sm["ids_ready"], 1)
            v.tensor_copy(ids[:], BANK_A[:, 0:SLOTS_W]).then_inc(sm["ids_taken"], 1)
            dve.wait_ge(sm["ids_taken"], 1)
            v.tensor_scalar(gather_i[:], ids[:], -1.0, 0.0, ALU.add, ALU.max).then_inc(sm["index_done"], 1)
            link(v.tensor_scalar(ids_pad[:], ids[:], 0.0, float(OUT_OF_BOUNDS), ALU.is_equal, ALU.mult))
            v.scalar_tensor_tensor(out=scatter_i[:], in0=ids[:], scalar=-1.0, in1=ids_pad[:],
                                   op0=ALU.add, op1=ALU.add).then_inc(sm["index_done"], 1)

            with nc.vector.register("slot_expert_dve") as reg:
                def take_xe(s, p):
                    dve.wait_ge(sm["xeT_ready"], s + 1)
                    v.tensor_copy(xeT[:, p], BANK_A[:, 0:D].rearrange("p (c s) -> p c s", c=KC))\
                        .then_inc(sm["xeT_taken"], 1)

                def take_h(s):
                    for c in range(2):
                        dve.wait_ge(sm["h_ready"], s * 2 + (c + 1))
                        v.tensor_copy(h_sb[:, 512 * c:512 * (c + 1)], S_BANK[c][:]).then_inc(sm["h_taken"], 1)

                def add_b2(s, p, j):
                    v.reg_load(reg, slot_e_i[0:1, bass.ds(s, 1)])
                    e = nc.s_assert_within(v.snap(reg), 0, E - 1)
                    dve.wait_ge(gathered_in[p], (j + 1) * 16)
                    v.tensor_tensor(x1_b2[:, p], gathered[:, p, 0:D], b2_sb[:, bass.ds(e * D, D)], ALU.add)\
                        .then_inc(sm["b2_done"], 1)

                def finish(s, p, j):
                    dve.wait_ge(sm["b2_done"], s + 1)
                    dve.wait_ge(sm["ye_ready"], s + 1)
                    if not (isinstance(j, int) and j == 0):
                        dve.wait_ge(y_out[p], j * 16)
                    v.tensor_tensor(y_sb[:, p], x1_b2[:, p], Y_BANK[p][:, 0:D], ALU.add)\
                        .then_inc(sm["ye_done"], 1)

                def turn(s, p, j, more=True):
                    take_h(s + 1)
                    finish(s, p, j)
                    if more:
                        take_xe(s + 2, p)
                        dve.wait_ge(sm["ye_done"], s + 1)
                        add_b2(s + 2, p, j + 1)

                dve.wait_ge(sm["b2_in"], 16)
                for s in range(2):
                    take_xe(s, s)
                    add_b2(s, s, 0)
                take_h(0)
                turn(0, 0, 0)
                turn(1, 1, 0)
                with dve.Fori(1, SLOTS // 2 - 1) as j:
                    turn(j * 2, 0, j)
                    turn(j * 2 + 1, 1, j)
                j = SLOTS // 2 - 1
                turn(j * 2, 0, j)
                turn(j * 2 + 1, 1, j, False)
                finish(SLOTS - 1, 0, j + 1)

        @block.tensor
        def _(pe):
            t = nc.tensor

            def project_k(b):
                pe.wait_ge(ctx_in[b.p], (b.half + 1) * 16)
                for m in range(KC):
                    for c in range(KC):
                        ins = t.matmul(BANK_B[:, P * m:P * (m + 1)], wk_sb[:, c, P * m:P * (m + 1)], ctx_sb[:, b.p, c],
                                       start=(c == 0), stop=(c == KC - 1))
                ins.then_inc(sm["k_ready"], 1)

            def project_v(b):
                for c in range(KC):
                    ins = t.matmul(BANK_B[:, 0:D], ctx_sb[:, b.p, c], wv_sb[:, c], start=(c == 0), stop=(c == KC - 1))
                ins.then_inc(sm["v_ready"], 1)

            def turn_x(b):
                pe.wait_ge(sm["xn_done"], b.n + 1)
                for c in range(KC):
                    ins = t.transpose(BANK_A[:, P * c:P * (c + 1)], xn[:, P * c:P * (c + 1)], ident[:])
                ins.then_inc(sm["xT_ready"], 1)

            def project_q(b):
                pe.wait_ge(sm["xT_taken"], b.n + 1)
                for m in range(KC):
                    for c in range(KC):
                        ins = t.matmul(BANK_A[:, P * m:P * (m + 1)], wq_sb[:, c, P * m:P * (m + 1)], xnT[:, c],
                                       start=(c == 0), stop=(c == KC - 1))
                ins.then_inc(sm["q_ready"], 1)

            def scores(b, qs):
                if qs[0] == 0:
                    pe.wait_ge(sm["q_stacked"], (b.n + 1) * STACKED)
                    pe.wait_ge(sm["k_stacked"], (b.n + 1) * STACKED)
                for q in qs:
                    if q == NQ - 1:
                        pe.wait_ge(sm["exp_done"], b.n * NQ + 1)
                    elif q == 0 and not (isinstance(b.n, int) and b.n == 0):
                        pe.wait_ge(sm["exp_done"], b.n * NQ)
                    for i in range(QUAD):
                        c, h = divmod(q * QUAD + i, HG)
                        ins = t.matmul(S_BANK[q % 3][:, P * i:P * (i + 1)], q_stack[0:SR, h, c], k_stack[0:SR, h, c],
                                       start=True, stop=True)
                    ins.then_inc(sm["scores_ready"], 1)

            def project_o(b):
                pe.wait_ge(sm["oT_done"], b.n + 1)
                for c in range(KC):
                    ins = t.matmul(BANK_A[:, 0:D], oT[:, b.p, c], wo_sb[:, c], start=(c == 0), stop=(c == KC - 1))
                ins.then_inc(sm["y_ready"], 1)

            def turn_x2(b):
                pe.wait_ge(sm["xn2_done"], b.n + 1)
                for c in range(KC):
                    ins = t.transpose(BANK_B[:, P * c:P * (c + 1)], record[:, b.p, D + P * c:D + P * (c + 1)], ident[:])
                ins.then_inc(sm["x2T_ready"], 1)

            def route(b):
                pe.wait_ge(sm["x2T_taken"], b.n + 1)
                for c in range(KC):
                    ins = t.matmul(BANK_A[:, 0:E], x2T[:, c], wr_sb[:, c], start=(c == 0), stop=(c == KC - 1))
                ins.then_inc(sm["logits_ready"], 1)

            def turn_probs(b, q):
                pe.wait_ge(sm["exp_done"], b.n * NQ + (q + 1))
                if not (isinstance(b.n, int) and b.n == 0 and q < 2):
                    pe.wait_ge(sm["probsT_taken"], b.n * NQ + q - 1)
                for i in range(QUAD):
                    ins = t.transpose(T_BANK[q % 2][:, P * i:P * (i + 1)], probs[:, QUAD * q + i], ident[:])
                ins.then_inc(sm["probsT_ready"], 1)

            def weigh_values(b, q):
                pe.wait_ge(sm["probsT_taken"], b.n * NQ + (q + 1))
                for i in range(QUAD):
                    c, h = divmod(q * QUAD + i, HG)
                    ins = t.matmul(O_BANK[:, P * c:P * (c + 1)], v_diag[:, b.p, c, h],
                                   probsT[:, q % 2, P * i:P * (i + 1)], start=(h == 0), stop=(h == HG - 1))
                ins.then_inc(sm["values_weighed"], 1)

            def turn_recips(b):
                pe.wait_ge(sm["recip_d_done"], b.n + 1)
                flat = recips_d[:].rearrange("p h d -> p (h d)")
                for c in range(KC):
                    ins = t.transpose(O_BANK[:, D + P * c:D + P * (c + 1)], flat[:, P * c:P * (c + 1)], ident[:])
                ins.then_inc(sm["rT_ready"], 1)

            def first():
                b = Batch(0, 0)
                pe.wait_ge(sm["wk_in"], 16)
                project_k(b)
                pe.wait_ge(sm["consts_pool"], 3)
                turn_x(b)
                pe.wait_ge(sm["wv_in"], 16)
                pe.wait_ge(sm["k_taken"], 1)
                project_v(b)
                pe.wait_ge(sm["wq_in"], 16)
                project_q(b)
                nxt = Batch(0, 1)
                pe.wait_ge(sm["v_taken"], 1)
                project_k(nxt)
                pe.wait_ge(sm["q_taken"], 1)
                turn_x(nxt)
                project_q(nxt)
                scores(b, range(NQ))
                pe.wait_ge(sm["wo_in"], 16)
                pe.wait_ge(sm["wr_in"], 16)

            def step(b, nxt, after, prev, before):
                start = b.n if isinstance(b.n, int) else NB
                turn_probs(b, 0)
                if nxt is not None:
                    if start < 3:
                        pe.wait_ge(sm["k_taken"], b.n + 2)
                    else:
                        pe.wait_ge(sm["x2T_taken"], b.n - 2)
                    project_v(nxt)
                turn_probs(b, 1)
                if prev is not None:
                    if start < 3:
                        pe.wait_ge(sm["q_taken"], b.n + 2)
                    else:
                        pe.wait_ge(sm["logits_taken"], b.n - 2)
                    project_o(prev)
                if prev is not None:
                    pe.wait_ge(sm["oT_done"], b.n)
                weigh_values(b, 0)
                turn_probs(b, 2)
                weigh_values(b, 1)
                if after is not None:
                    if prev is None:
                        pe.wait_ge(sm["q_taken"], b.n + 2)
                    else:
                        pe.wait_ge(sm["x1_done"], b.n)
                    turn_x(after)
                turn_probs(b, 3)
                if after is not None:
                    pe.wait_ge(sm["v_taken"], nxt.n + 1)
                    project_k(after)
                if nxt is not None:
                    scores(nxt, EARLY)
                if after is not None:
                    project_q(after)
                weigh_values(b, 2)
                if before is not None:
                    if after is not None:
                        pe.wait_ge(sm["k_taken"], after.n + 1)
                    elif nxt is not None:
                        pe.wait_ge(sm["v_taken"], nxt.n + 1)
                    else:
                        pe.wait_ge(sm["x2T_taken"], b.n - 2)
                    turn_x2(before)
                weigh_values(b, 3)
                turn_recips(b)
                if nxt is not None:
                    scores(nxt, [NQ - 1])
                if before is not None:
                    if after is not None:
                        pe.wait_ge(sm["q_taken"], after.n + 1)
                    else:
                        pe.wait_ge(sm["x1_done"], b.n)
                    route(before)

            def last(prev, b):
                pe.wait_ge(sm["logits_taken"], prev.n)
                project_o(b)
                pe.wait_ge(sm["x2T_taken"], prev.n)
                turn_x2(prev)
                pe.wait_ge(sm["x1_done"], b.n + 1)
                route(prev)
                pe.wait_ge(sm["x2T_taken"], b.n)
                turn_x2(b)
                pe.wait_ge(sm["logits_taken"], b.n)
                route(b)

            steps(pe, first, step, last)

            pe.wait_ge(sm["onehot_done"], 1)
            t.matmul(BANK_B[:, 0:NB * E], earlier[:], onehot[:].rearrange("p b e -> p (b e)"), start=True, stop=False)
            for b in range(NB):
                ins = t.matmul(BANK_A[:, 0:E], ones[:], onehot[:, b], start=(b == 0), stop=(b == NB - 1))
            ins.then_inc(sm["total_ready"], 1)
            for b in range(NB - 1):
                ins = t.matmul(BANK_B[:, E * (b + 1):E * NB], ones[:],
                               onehot[:, b:b + 1].broadcast_to([P, NB - 1 - b, E]), start=False, stop=(b == NB - 2))
            ins.then_inc(sm["rank_ready"], 1)
            for b in range(NB):
                if b < DVE_ROWS:
                    pe.wait_ge(sm["code_tok_dve"], b + 1)
                else:
                    pe.wait_ge(sm["code_tok_pool"], b + 1 - DVE_ROWS)
                pe.wait_ge(sm["place_hot_done"], b + 1)
                ins = t.matmul(BANK_B[:, 0:P], code_tok[:, b], place_hot[:, b], start=(b == 0), stop=(b == NB - 1))
            ins.then_inc(sm["ids_T_ready"], 1)
            pe.wait_ge(sm["ids_T_done"], 1)
            pe.wait_ge(sm["code_hot_done"], 1)
            t.matmul(BANK_A[:, 0:SLOTS_W], ids_T[:], code_hot[:], start=True, stop=True).then_inc(sm["ids_ready"], 1)

            pe.wait_ge(sm["w1_in"], 16 * E)
            pe.wait_ge(sm["w2_in"], 16 * E)
            pe.wait_ge(sm["ids_taken"], 1)
            pe.wait_ge(sm["slots_done"], 1)

            def turn_xe(s, p, j):
                pe.wait_ge(gathered_in[p], (j + 1) * 16)
                if not (isinstance(s, int) and s == 0):
                    pe.wait_ge(sm["xeT_taken"], s)
                for c in range(KC):
                    ins = t.transpose(BANK_A[:, P * c:P * (c + 1)], gathered[:, p, D + P * c:D + P * (c + 1)], ident[:])
                ins.then_inc(sm["xeT_ready"], 1)

            def up(s, p, e):
                pe.wait_ge(sm["xeT_taken"], s + 1)
                for n in range(2):
                    for c in range(KC):
                        ins = t.matmul(S_BANK[n][:], xeT[:, p, c],
                                       w1_flat[:, bass.ds(e * (KC * F) + (c * F + 512 * n), 512)],
                                       start=(c == 0), stop=(c == KC - 1))
                    ins.then_inc(sm["h_ready"], 1)

            def turn_h(s):
                for c in range(FC):
                    if c % 4 == 0:
                        pe.wait_ge(sm["h_taken"], s * 2 + (c // 4 + 1))
                    ins = t.transpose(T_BANK[c // 4][:, P * (c % 4):P * (c % 4 + 1)], h_sb[:, P * c:P * (c + 1)],
                                      ident[:])
                    if c % 4 == 3:
                        ins.then_inc(sm["hT_ready"], 1)

            def down(s, p, e):
                for c in range(FC):
                    if c % 4 == 0:
                        pe.wait_ge(sm["gelu_done"], s * 2 + (c // 4 + 1))
                    ins = t.matmul(Y_BANK[p][:, 0:D], hT[:, c],
                                   w2_flat[:, bass.ds(e * (FC * D) + c * D, D)],
                                   start=(c == 0), stop=(c == FC - 1))
                ins.then_inc(sm["ye_ready"], 1)

            w1_flat = w1_sb[:].rearrange("p e c f -> p (e c f)")
            w2_flat = w2_sb[:].rearrange("p e c d -> p (e c d)")
            with nc.tensor.register("slot_expert_0") as reg0, nc.tensor.register("slot_expert_1") as reg1:
                def expert_of(reg, s):
                    t.reg_load(reg, slot_e_i[0:1, bass.ds(s, 1)])
                    return nc.s_assert_within(t.snap(reg), 0, E - 1)

                turn_xe(0, 0, 0)
                turn_xe(1, 1, 0)
                up(0, 0, expert_of(reg0, 0))
                turn_h(0)
                assert SLOTS % 2 == 1
                with pe.Fori(0, SLOTS // 2 - 1) as j:
                    s = j * 2
                    up(s + 1, 1, expert_of(reg1, s + 1))
                    down(s, 0, expert_of(reg0, s))
                    turn_xe(s + 2, 0, j + 1)
                    turn_h(s + 1)
                    up(s + 2, 0, expert_of(reg0, s + 2))
                    down(s + 1, 1, expert_of(reg1, s + 1))
                    turn_xe(s + 3, 1, j + 1)
                    turn_h(s + 2)
                s = SLOTS - 3
                up(s + 1, 1, expert_of(reg1, s + 1))
                down(s, 0, expert_of(reg0, s))
                turn_xe(s + 2, 0, s // 2 + 1)
                turn_h(s + 1)
                up(s + 2, 0, expert_of(reg0, s + 2))
                down(s + 1, 1, expert_of(reg1, s + 1))
                turn_h(s + 2)
                down(s + 2, 0, expert_of(reg0, s + 2))


def kernel(x, ctx_1024, L0_xattn_Wq, L0_xattn_bq, L0_xattn_Wk, L0_xattn_bk, L0_xattn_Wv, L0_xattn_bv, L0_xattn_Wo,
           L0_xattn_bo, L0_ffn_wr, L0_ffn_br, L0_ffn_w1, L0_ffn_b1, L0_ffn_w2, L0_ffn_b2):
    import numpy as np
    import concourse.bacc as bacc
    from concourse.bass_utils import run_bass_kernel_spmd as run

    x = np.asarray(x)
    E, F = np.asarray(L0_ffn_b1).shape
    arrays = {
        "x": x,
        "ctxT": np.asarray(ctx_1024).transpose(0, 2, 1),
        "wqT": np.asarray(L0_xattn_Wq).T, "bqT": np.asarray(L0_xattn_bq).reshape(-1, 128).T,
        "wkT": np.asarray(L0_xattn_Wk).T, "bkT": np.asarray(L0_xattn_bk).reshape(-1, 128).T,
        "wvT": np.asarray(L0_xattn_Wv).T, "bv": L0_xattn_bv,
        "woT": np.asarray(L0_xattn_Wo).T, "bo": L0_xattn_bo,
        "wr": L0_ffn_wr, "br": L0_ffn_br,
        "w1": L0_ffn_w1, "b1T": np.asarray(L0_ffn_b1).reshape(E * F // 128, 128).T,
        "w2": L0_ffn_w2, "b2": np.asarray(L0_ffn_b2).reshape(-1),
    }
    arrays = {k: np.ascontiguousarray(v) for k, v in arrays.items()}
    nc = bacc.Bacc("TRN2", target_bir_lowering=False, num_devices=1)
    args = [nc.dram_tensor(f"in_{k}", v.shape, F32, kind="ExternalInput").ap() for k, v in arrays.items()]
    out = nc.dram_tensor("out", [x.shape[0] * x.shape[1], x.shape[2]], F32, kind="ExternalOutput").ap()
    cross_attention_moe_kernel(nc, *args, out)
    r = run(nc, [{f"in_{k}": v for k, v in arrays.items()}], core_ids=[0])
    return r.results[0]["out"].reshape(x.shape)
```
